# Optimizing a Trainium2 kernel written in Bass

```python
import numpy as np
import jax
import jax.numpy as jnp

def _softmax(x, axis=-1):
    return jax.nn.softmax(x, axis=axis)

def _gelu(x):
    return jax.nn.gelu(x, approximate=True)

def _silu(x):
    return jax.nn.silu(x)

def _sigmoid(x):
    return jax.nn.sigmoid(x)

def _layernorm(x, axis=-1, eps=1e-05):
    m = jnp.mean(x, axis=axis, keepdims=True)
    v = jnp.var(x, axis=axis, keepdims=True)
    return (x - m) / jnp.sqrt(v + eps)

def _scatter_add(tgt, idx, src, axis=0):
    return tgt.at[idx].add(src)

def _segment_sum(src, seg, n):
    return jax.ops.segment_sum(src, seg, n)
kernel_name = 'mk_gnn_preln_d4_gnn_r8_73d48a'

def setup_inputs(seed: int=0):
    np.random.seed(seed)
    _w = jnp.asarray

    def _rec_inputs():
        import jax
        import jax.numpy as jnp
        _gk = jax.random.key(seed)
        x = -0.000202 + 1 * jax.random.normal(jax.random.fold_in(_gk, 1), (6250, 64), jnp.float32)
        src = jax.random.randint(jax.random.fold_in(_gk, 2), (200000,), 0, 6250, jnp.int32)
        dst = jnp.minimum((6250 * jax.random.uniform(jax.random.fold_in(_gk, 3), (200000,)) ** 2.0).astype(jnp.int32), 49999)
        _o = jnp.argsort(dst, stable=True)
        src = src[_o]
        dst = dst[_o]
        edge_attr_64 = -8.47137e-05 + 0.99988 * jax.random.normal(jax.random.fold_in(_gk, 11), (200000, 64), jnp.float32)
        edge_weight = jax.random.uniform(jax.random.fold_in(_gk, 14), (200000,), jnp.float32, 0.0, 0.999999)
        return (x, src, dst, edge_attr_64, edge_weight)
    x, src, dst, edge_attr_64, edge_weight = _rec_inputs()

    def _L0_gnn_setup():
        import jax, jax.numpy as jnp
        import numpy as np
        D = 64
        N_ATOMS = 12500
        N_BONDS = 187500

        def _gated_mlp(x, W1, b1, W2, b2, G1, g1, G2, g2):
            h = jax.nn.silu(x @ W1 + b1)
            h = jax.nn.silu(h @ W2 + b2)
            g = jax.nn.silu(x @ G1 + g1)
            g = jax.nn.sigmoid(g @ G2 + g2)
            return h * g
        key = jax.random.key(seed)
        ks = jax.random.split(key, 8)
        s = 1.0 / np.sqrt(D)
        return {'atom_features': jax.random.normal(ks[0], (N_ATOMS, D), jnp.float32), 'bond_features': jax.random.normal(ks[1], (N_BONDS, D), jnp.float32), 'W1': jax.random.normal(ks[2], (D, D), jnp.float32) * s, 'b1': jnp.zeros((D,), jnp.float32), 'W2': jax.random.normal(ks[3], (D, D), jnp.float32) * s, 'b2': jnp.zeros((D,), jnp.float32), 'G1': jax.random.normal(ks[4], (D, D), jnp.float32) * s, 'g1': jnp.zeros((D,), jnp.float32), 'G2': jax.random.normal(ks[5], (D, D), jnp.float32) * s, 'g2': jnp.zeros((D,), jnp.float32), 'bond_atom_indices': jax.random.randint(ks[6], (N_BONDS, 2), 0, N_ATOMS, jnp.int32)}
    _L0_gnn_all = _L0_gnn_setup()
    _L0_gnn_in = {k: v for k, v in _L0_gnn_all.items() if k in ('W1', 'b1', 'W2', 'b2', 'G1', 'g1', 'G2', 'g2')}
    del _L0_gnn_all

    def _L1_gnn_setup():
        import jax, jax.numpy as jnp
        import numpy as np
        N_NODES = 12500
        N_EDGES = 160000
        IN_CH = 64
        OUT_CH = 64
        key = jax.random.key(seed)
        k1, k2, k3 = jax.random.split(key, 3)
        x = jax.random.normal(k1, (N_NODES, IN_CH), dtype=jnp.float32)
        edge_index = jax.random.randint(k2, (2, N_EDGES), 0, N_NODES, dtype=jnp.int32)
        W = jax.random.normal(k3, (IN_CH, OUT_CH), dtype=jnp.float32) * (1.0 / np.sqrt(IN_CH))
        b = jnp.zeros((OUT_CH,), dtype=jnp.float32)
        return {'x': x, 'edge_index': edge_index, 'W': W, 'b': b}
    _L1_gnn_all = _L1_gnn_setup()
    _L1_gnn_in = {k: v for k, v in _L1_gnn_all.items() if k in ('W', 'b')}
    del _L1_gnn_all

    def _L2_gnn_setup():
        import jax, jax.numpy as jnp
        import numpy as np
        N_NODES = 12500
        N_EDGES = 200000
        D_IN = 64
        D_OUT = 64
        key = jax.random.key(seed)
        k1, k2, k3, k4 = jax.random.split(key, 4)
        x = jax.random.normal(k1, (N_NODES, D_IN), dtype=jnp.float32)
        edge_index = jax.random.randint(k2, (2, N_EDGES), 0, N_NODES, dtype=jnp.int64)
        edge_weight = jax.random.uniform(k3, (N_EDGES,), dtype=jnp.float32)
        W = jax.random.normal(k4, (D_OUT, D_IN), dtype=jnp.float32) * (1.0 / np.sqrt(D_IN))
        b = jnp.zeros((D_OUT,), dtype=jnp.float32)
        return {'x': x, 'edge_index': edge_index, 'edge_weight': edge_weight, 'W': W, 'b': b}
    _L2_gnn_all = _L2_gnn_setup()
    _L2_gnn_in = {k: v for k, v in _L2_gnn_all.items() if k in ('W', 'b')}
    del _L2_gnn_all

    def _L3_gnn_setup():
        import jax, jax.numpy as jnp
        import numpy as np
        N_NODES = 12500
        N_EDGES = 150000
        D_IN = 64
        D_HID = 64

        def _mean_aggregate(x, src, dst, n_nodes):
            msg = x[src]
            summed = jax.ops.segment_sum(msg, dst, num_segments=n_nodes)
            deg = jax.ops.segment_sum(jnp.ones((src.shape[0],), dtype=x.dtype), dst, num_segments=n_nodes)
            return summed / jnp.maximum(deg, 1.0)[:, None]

        def _sage_conv(x, src, dst, Wl, bl, Wr):
            agg = _mean_aggregate(x, src, dst, x.shape[0])
            return agg @ Wl + bl + x @ Wr
        key = jax.random.key(seed)
        ks = jax.random.split(key, 8)
        x = jax.random.normal(ks[0], (N_NODES, D_IN), dtype=jnp.float32)
        edge_index = jax.random.randint(ks[1], (2, N_EDGES), 0, N_NODES, dtype=jnp.int64)
        s = 1.0 / np.sqrt(D_IN)
        Wl0 = jax.random.normal(ks[2], (D_IN, D_HID), dtype=jnp.float32) * s
        bl0 = jax.random.normal(ks[3], (D_HID,), dtype=jnp.float32) * s
        Wr0 = jax.random.normal(ks[4], (D_IN, D_HID), dtype=jnp.float32) * s
        Wl1 = jax.random.normal(ks[5], (D_HID, D_HID), dtype=jnp.float32) * s
        bl1 = jax.random.normal(ks[6], (D_HID,), dtype=jnp.float32) * s
        Wr1 = jax.random.normal(ks[7], (D_HID, D_HID), dtype=jnp.float32) * s
        return {'x': x, 'edge_index': edge_index, 'Wl0': Wl0, 'bl0': bl0, 'Wr0': Wr0, 'Wl1': Wl1, 'bl1': bl1, 'Wr1': Wr1}
    _L3_gnn_all = _L3_gnn_setup()
    _L3_gnn_in = {k: v for k, v in _L3_gnn_all.items() if k in ('Wl0', 'bl0', 'Wr0', 'Wl1', 'bl1', 'Wr1')}
    del _L3_gnn_all
    return {'x': x, 'src': src, 'dst': dst, 'edge_attr_64': edge_attr_64, 'edge_weight': edge_weight, 'L0_gnn_W1': _L0_gnn_in['W1'], 'L0_gnn_b1': _L0_gnn_in['b1'], 'L0_gnn_W2': _L0_gnn_in['W2'], 'L0_gnn_b2': _L0_gnn_in['b2'], 'L0_gnn_G1': _L0_gnn_in['G1'], 'L0_gnn_g1': _L0_gnn_in['g1'], 'L0_gnn_G2': _L0_gnn_in['G2'], 'L0_gnn_g2': _L0_gnn_in['g2'], 'L1_gnn_W': _L1_gnn_in['W'], 'L1_gnn_b': _L1_gnn_in['b'], 'L2_gnn_W': _L2_gnn_in['W'], 'L2_gnn_b': _L2_gnn_in['b'], 'L3_gnn_Wl0': _L3_gnn_in['Wl0'], 'L3_gnn_bl0': _L3_gnn_in['bl0'], 'L3_gnn_Wr0': _L3_gnn_in['Wr0'], 'L3_gnn_Wl1': _L3_gnn_in['Wl1'], 'L3_gnn_bl1': _L3_gnn_in['bl1'], 'L3_gnn_Wr1': _L3_gnn_in['Wr1']}

def reference(x, src, dst, edge_attr_64, edge_weight, L0_gnn_W1, L0_gnn_b1, L0_gnn_W2, L0_gnn_b2, L0_gnn_G1, L0_gnn_g1, L0_gnn_G2, L0_gnn_g2, L1_gnn_W, L1_gnn_b, L2_gnn_W, L2_gnn_b, L3_gnn_Wl0, L3_gnn_bl0, L3_gnn_Wr0, L3_gnn_Wl1, L3_gnn_bl1, L3_gnn_Wr1):
    import jax
    import jax.numpy as jnp

    def _L0_gnn_ref(atom_features, bond_features, W1, b1, W2, b2, G1, g1, G2, g2, bond_atom_indices):
        import jax, jax.numpy as jnp
        import numpy as np
        D = 64
        N_ATOMS = 12500
        N_BONDS = 187500

        def _gated_mlp(x, W1, b1, W2, b2, G1, g1, G2, g2):
            h = jax.nn.silu(x @ W1 + b1)
            h = jax.nn.silu(h @ W2 + b2)
            g = jax.nn.silu(x @ G1 + g1)
            g = jax.nn.sigmoid(g @ G2 + g2)
            return h * g
        messages = _gated_mlp(bond_features, W1, b1, W2, b2, G1, g1, G2, g2)
        recv = bond_atom_indices[:, 1]
        summed = jax.ops.segment_sum(messages, recv, num_segments=atom_features.shape[0])
        return atom_features + summed

    def _L1_gnn_ref(x, edge_index, W, b):
        import jax, jax.numpy as jnp
        import numpy as np
        N_NODES = 12500
        N_EDGES = 160000
        IN_CH = 64
        OUT_CH = 64
        n = x.shape[0]
        self_loops = jnp.arange(n, dtype=edge_index.dtype)
        src = jnp.concatenate([edge_index[0], self_loops])
        dst = jnp.concatenate([edge_index[1], self_loops])
        deg = jnp.zeros((n,), dtype=x.dtype).at[dst].add(1.0)
        deg_inv_sqrt = jnp.where(deg > 0, jax.lax.rsqrt(deg), 0.0)
        norm = deg_inv_sqrt[src] * deg_inv_sqrt[dst]
        h = x @ W
        msg = h[src] * norm[:, None]
        agg = jax.ops.segment_sum(msg, dst, num_segments=n)
        return jax.nn.relu(agg + b)

    def _L2_gnn_ref(x, edge_index, edge_weight, W, b):
        import jax, jax.numpy as jnp
        import numpy as np
        N_NODES = 12500
        N_EDGES = 200000
        D_IN = 64
        D_OUT = 64
        N = x.shape[0]
        loop = jnp.arange(N, dtype=edge_index.dtype)
        row = jnp.concatenate([edge_index[0], loop])
        col = jnp.concatenate([edge_index[1], loop])
        w = jnp.concatenate([edge_weight, jnp.ones((N,), dtype=x.dtype)])
        deg = jax.ops.segment_sum(w, row, num_segments=N)
        safe = jnp.where(deg > 0, deg, 1.0)
        dinv = jnp.where(deg > 0, safe ** (-0.5), 0.0)
        norm_w = dinv[row] * w * dinv[col]
        agg = jax.ops.segment_sum(norm_w[:, None] * x[col], row, num_segments=N)
        return agg @ W.T + b

    def _L3_gnn_ref(x, edge_index, Wl0, bl0, Wr0, Wl1, bl1, Wr1):
        import jax, jax.numpy as jnp
        import numpy as np
        N_NODES = 12500
        N_EDGES = 150000
        D_IN = 64
        D_HID = 64

        def _mean_aggregate(x, src, dst, n_nodes):
            msg = x[src]
            summed = jax.ops.segment_sum(msg, dst, num_segments=n_nodes)
            deg = jax.ops.segment_sum(jnp.ones((src.shape[0],), dtype=x.dtype), dst, num_segments=n_nodes)
            return summed / jnp.maximum(deg, 1.0)[:, None]

        def _sage_conv(x, src, dst, Wl, bl, Wr):
            agg = _mean_aggregate(x, src, dst, x.shape[0])
            return agg @ Wl + bl + x @ Wr
        src, dst = (edge_index[0], edge_index[1])
        h = _sage_conv(x, src, dst, Wl0, bl0, Wr0)
        h = jax.nn.relu(h)
        h = _sage_conv(h, src, dst, Wl1, bl1, Wr1)
        return h
    edge_index = jnp.stack([src, dst])
    edge_index_t = jnp.stack([src, dst], axis=1)
    h = jnp.maximum(_layernorm(x, axis=-1), 0.0)
    x = x + _L0_gnn_ref(h, edge_attr_64, L0_gnn_W1, L0_gnn_b1, L0_gnn_W2, L0_gnn_b2, L0_gnn_G1, L0_gnn_g1, L0_gnn_G2, L0_gnn_g2, edge_index_t)
    h = jnp.maximum(_layernorm(x, axis=-1), 0.0)
    x = x + _L1_gnn_ref(h, edge_index, L1_gnn_W, L1_gnn_b)
    h = jnp.maximum(_layernorm(x, axis=-1), 0.0)
    x = x + _L2_gnn_ref(h, edge_index, edge_weight, L2_gnn_W, L2_gnn_b)
    h = jnp.maximum(_layernorm(x, axis=-1), 0.0)
    x = x + _L3_gnn_ref(h, edge_index, L3_gnn_Wl0, L3_gnn_bl0, L3_gnn_Wr0, L3_gnn_Wl1, L3_gnn_bl1, L3_gnn_Wr1)
    return x

_drawn_inputs = setup_inputs


def setup_inputs(seed=0):
    import zlib

    import numpy as np

    out = dict(_drawn_inputs(seed))
    spreads = {'L0_gnn_b1': (0.0, 0.1),
     'L0_gnn_b2': (0.0, 0.1),
     'L0_gnn_g1': (0.0, 0.288),
     'L0_gnn_g2': (0.0, 0.1),
     'L1_gnn_b': (0.0, 0.444),
     'L2_gnn_b': (0.0, 0.359)}
    factors = {'edge_weight': 5.022}
    for name, (base, spread) in spreads.items():
        noise = np.random.default_rng([zlib.crc32(name.encode()), seed]).standard_normal(out[name].shape)
        drawn = base * np.exp(spread * noise) if base else spread * noise
        out[name] = jnp.asarray(drawn.astype(out[name].dtype))
    for name, factor in factors.items():
        out[name] = (out[name] * factor).astype(out[name].dtype)
    return out
```

```python
import concourse.bass as bass
from concourse import mybir
from contextlib import ExitStack

P = 128
N_NODES, N_EDGES, D = 6250, 200000, 64
NW = -(-N_NODES // P)
NWP = NW + NW % 2
NODES = NW * P
DUMMY = NODES - 1
CH = 512
R = 8
EDGES = -(-N_EDGES // (R * P)) * R * P
TILES = EDGES // P
CHUNKS = EDGES // CH
QT = CH // P
CSTEPS = CHUNKS + NW - 1
TSTEPS = TILES + NW - 1
R0 = 4
MW = D + 1
EPS = 1e-5


def ds(start, size):
    return bass.DynSlice(start, size)


def wait(eng, sem, value):
    if not isinstance(value, int) or value > 0:
        eng.wait_ge(sem, value)


def gnn_kernel(nc, x, edge_t, dst_tiles, src_tiles, src_rows, dst_rows, w_rows, w1g1, w2g2, b1g1, b2g2,
               w_gcn, w_l2, w_l0, w_r0, w_l1, w_r1, b_gcn, b_l2, b_l0, b_l1, out):
    f32, bf16, i32 = mybir.dt.float32, mybir.dt.bfloat16, mybir.dt.int32
    ALU, ACT, AX = mybir.AluOpType, mybir.ActivationFunctionType, mybir.AxisListType
    ctx = ExitStack()
    with ctx:
        def sb(name, shape, dt=f32):
            return ctx.enter_context(nc.sbuf_tensor(name, shape, dt))

        def sem(name):
            return ctx.enter_context(nc.semaphore(name))

        records = nc.dram_tensor("records", (EDGES, 4), i32).ap()
        table = nc.dram_tensor("table", (NODES, D), f32).ap()

        X = sb("X", [P, NWP, D])
        H = sb("H", [P, NWP, D])
        ACC = sb("ACC", [P, NWP, MW])
        S1 = sb("S1", [P, NWP, D])
        S2 = sb("S2", [P, NWP, D])
        count = sb("count", [P, NWP])
        scale1 = sb("scale1", [P, NWP])
        scale2 = sb("scale2", [P, NWP])
        scale3 = sb("scale3", [P, NWP])
        mean = sb("mean", [P, NWP])
        rstd = sb("rstd", [P, NWP])
        iota_all = sb("iota_all", [P, NODES])
        dst_f = sb("dst_f", [P, TILES])
        src_i = sb("src_i", [P, TILES], i32)
        rec = sb("rec", [P, TILES, 4], i32)
        recf = rec[:, :, :].bitcast(f32)
        srt_f = sb("srt_f", [P, TILES])
        hi_f = sb("hi_f", [P, TILES])
        lo_f = sb("lo_f", [P, TILES])
        slot_i = sb("slot_i", [P, TILES], i32)
        s1v = S1[:, :, :].rearrange("p a b -> p (a b)")
        s2v = S2[:, :, :].rearrange("p a b -> p (a b)")
        accv = ACC[:, :, :].rearrange("p a b -> p (a b)")
        srow_i = s1v[:, 0:TILES].bitcast(i32)
        drow_i = s1v[:, TILES:2 * TILES].bitcast(i32)
        wrow = s2v[:, 0:TILES]
        mask = s2v[:, TILES:2 * TILES]
        run = srt_f[:, :]
        pos = accv[:, 0:TILES]
        tmp_i = accv[:, TILES:2 * TILES].bitcast(i32)
        dtile_i = slot_i
        ident = sb("ident", [P, P])
        before = sb("before", [P, P])
        ones = sb("ones", [P, P])
        wcol = sb("wcol", [P, NW])
        pidx = sb("pidx", [P, 1])
        cnt = sb("cnt", [P, 2, NW])
        cex = sb("cex", [P, 2, NW])
        base = sb("base", [P, NW])
        wst_i = sb("wst_i", [NW, 4], i32)
        wst = sb("wst", [NW, 4])
        dwin_c = sb("dwin_c", [1, CSTEPS], i32)
        dwin_t = sb("dwin_t", [1, TSTEPS], i32)
        swin_t = sb("swin_t", [1, TSTEPS], i32)
        w1s = sb("w1s", [P, P])
        w2s = sb("w2s", [P, P])
        b1s = sb("b1s", [P, 1])
        b2s = sb("b2s", [1, CH])
        wns = [sb(f"wn{i}", [P, P]) for i in range(6)]
        bns = [sb(f"bn{i}", [P, D]) for i in range(4)]
        ring = sb("ring", [P, R0 * CH])
        xs = ring[:, 0:2 * CH].rearrange("p (r e) -> p r e", r=R0)
        h1 = ring[:, 2 * CH:4 * CH].rearrange("p (r e) -> p r e", r=2)
        at = ring[:, :].rearrange("p (a b e) -> p a b e", a=2, b=2)
        sl = sb("sl", [P, 2, QT, D])
        th = sb("th", [P, 2, QT, D])
        msg = sb("msg", [P, 2, QT, MW])
        oh0 = sb("oh0", [P, 2, QT, P])
        idx_s = sb("idx_s", [P, R], i32)
        rec_s = sb("rec_s", [P, R, 4], i32)
        got = sb("got", [P, R, D])
        oh = sb("oh", [P, R, P])
        ohd = sb("ohd", [P, 4, P])
        ohw = sb("ohw", [P, 4, NW])
        ps = ctx.enter_context(nc.psum_tensor("ps", [P, 8, 512], f32))

        s_w, s_x, s_dt, s_st, s_rows = sem("s_w"), sem("s_x"), sem("s_dt"), sem("s_st"), sem("s_rows")
        s_const, s_pc = sem("s_const"), sem("s_pc")
        s_v = sem("s_v")
        s_cnt, s_tot, s_wst, s_wind, s_wsum, s_win = (sem(n) for n in ("s_cnt", "s_tot", "s_wst", "s_wind", "s_wsum", "s_win"))
        s_slot, s_stg, s_sc = sem("s_slot"), sem("s_stg"), [sem(f"s_sc{i}") for i in range(R)]
        s_xc = [sem(f"s_xc{i}") for i in range(R0)]
        s_mm1, s_h1, s_mm2, s_sl, s_msg, s_oh0, s_scat, s_acc = (sem(n) for n in (
            "s_mm1", "s_h1", "s_mm2", "s_sl", "s_msg", "s_oh0", "s_scat", "s_acc"))
        s_do, s_dm = sem("s_do"), sem("s_dm")
        s_rec = sem("s_rec")
        s_idx, s_oh, s_mm, s_add = sem("s_idx"), sem("s_oh"), sem("s_mm"), sem("s_add")
        s_g = [sem(f"s_g{i}") for i in range(R)]
        s_begun, s_placed = sem("s_begun"), sem("s_placed")
        s_var, s_std = sem("s_var"), sem("s_std")
        s_op, s_tp, s_at, s_y, s_ev = sem("s_op"), sem("s_tp"), sem("s_at"), sem("s_y"), sem("s_ev")
        s_tab, s_tst, s_fin, s_out = sem("s_tab"), sem("s_tst"), sem("s_fin"), sem("s_out")
        block = ctx.enter_context(nc.Block())

        N_WEIGHTS = 4 + 6 + 4
        PASSES = 4
        GROUPS = [list(range(g, min(g + 4, NWP // 2))) for g in range(0, NWP // 2, 4)]
        LINEARS = [1, 1, 2, 2]

        def window_of(eng, tab, s):
            return nc.values_load(tab[0:1, ds(s, 1)], engines=[eng.engine], min_val=0, max_val=NW - 1,
                                  skip_runtime_bounds_check_because="a count of 49 windows, less one, the first of which has always begun")

        def window(eng, tab, s, nsteps):
            v = window_of(eng, tab, s)
            return v, nc.s_assert_within(s - v, 0, nsteps - NW, skip_runtime_bounds_check_because="window w begins w steps or more after the first, and is on the last tile at most w steps before the end")

        @block.sync
        def _(sp):
            sp.dma_start(srow_i, src_rows).then_inc(s_rows, 16)
            sp.dma_start(drow_i, dst_rows).then_inc(s_rows, 16)
            sp.dma_start(wrow, w_rows).then_inc(s_rows, 16)
            sp.dma_start(X[:, :, :], x).then_inc(s_x, 16)
            sp.dma_start(dtile_i[:, :], dst_tiles).then_inc(s_dt, 16)
            sp.dma_start(src_i[:, :], src_tiles).then_inc(s_st, 16)
            for to, of in [(w1s, w1g1), (w2s, w2g2), (b1s, b1g1), (b2s, b2g2)] + list(
                    zip(wns, (w_gcn, w_l2, w_l0, w_r0, w_l1, w_r1))) + list(zip(bns, (b_gcn, b_l2, b_l0, b_l1))):
                sp.dma_start(to[:, :], of).then_inc(s_w, 16)
            sp.wait_ge(s_win, 3)

            def chunk(s, u):
                w, c = window(sp, dwin_c, s, CSTEPS)
                wait(sp, s_mm1, s - R0 + 1)
                sp.dma_start(xs[:, u, :], edge_t[ds(c, 1), :, :].rearrange("a p e -> (a p) e")).then_inc(s_xc[u], 16)

            for s in range(R0):
                chunk(s, s)
            with sp.Fori(1, CSTEPS // R0, 1) as i:
                for u in range(R0):
                    chunk(i * R0 + u, u)
            for u in range(R):
                sp.wait_ge(s_sc[u], 16 * (TILES // R))
            sp.wait_ge(s_dm, TILES)
            sp.dma_start(rec[:, :, :], records.rearrange("(p t) k -> p t k", p=P)).then_inc(s_rec, 16)
            for k in range(PASSES):
                sp.wait_ge(s_tab, k + 1)
                of = [S1, S1, H, H][k]
                sp.dma_start(table.rearrange("(w p) f -> p w f", p=P), of[:, 0:NW, :]).then_inc(s_tst, 16)
            sp.wait_ge(s_fin, 1)
            full = N_NODES // P
            sp.dma_start(out[0:full * P, :].rearrange("(w p) f -> p w f", p=P), X[:, 0:full, :]).then_inc(s_out, 16)
            sp.dma_start(out[full * P:N_NODES, :], X[0:N_NODES - full * P, full, :]).then_inc(s_out, 16)
            sp.wait_ge(s_out, 32)

        @block.gpsimd
        def _(pool):
            nc.gpsimd.iota(iota_all[:, :], [[1, NODES]], base=0, channel_multiplier=0,
                           allow_small_or_imprecise_dtypes=True).then_inc(s_const, 1)
            nc.gpsimd.iota(wcol[:, :], [[1, NW]], base=0, channel_multiplier=0,
                           allow_small_or_imprecise_dtypes=True).then_inc(s_const, 1)
            nc.gpsimd.iota(pidx[:, :], [[0, 1]], base=0, channel_multiplier=1,
                           allow_small_or_imprecise_dtypes=True).then_inc(s_const, 1)
            nc.gpsimd.memset(ones[:, :], 1.0).then_inc(s_const, 1)
            nc.gpsimd.memset(ident[:, :], 0.0).then_inc(s_pc, 1)
            nc.gpsimd.memset(before[:, :], 1.0).then_inc(s_pc, 1)
            pool.wait_ge(s_pc, 2)
            nc.gpsimd.affine_select(out=ident[:, :], in_=ident[:, :], compare_op=ALU.not_equal, fill=1.0,
                                    base=0, pattern=[[-1, P]], channel_multiplier=1).then_inc(s_const, 1)
            nc.gpsimd.affine_select(out=before[:, :], in_=before[:, :], compare_op=ALU.is_gt, fill=0.0,
                                    base=0, pattern=[[1, P]], channel_multiplier=-1).then_inc(s_const, 1)
            pool.wait_ge(s_slot, 1)

            def scatter(i):
                if not isinstance(i, int):
                    for u in range(R):
                        pool.wait_ge(s_sc[u], i * 16)
                nc.gpsimd.tensor_copy(idx_s[:, :], slot_i[:, ds(i * R, R)]).then_inc(s_stg, 1)
                nc.gpsimd.tensor_copy(rec_s[:, :, :], rec[:, ds(i * R, R), :]).then_inc(s_stg, 1)
                pool.wait_ge(s_stg, i * 2 + 2)
                pool.sem_inc(s_begun, 1)
                for u in range(R):
                    pool.indirect_dma_start(records, bass.IndirectOffsetOnAxis(ap=idx_s[:, u:u + 1], axis=0),
                                            rec_s[:, u, :], None).then_inc(s_sc[u], 16)

            scatter(0)
            with pool.Fori(1, TILES // R, 1) as i:
                scatter(i)

            def gather(k, s, u):
                pool.wait_ge(s_idx, k * TSTEPS + s + 1)
                wait(pool, s_mm, k * TSTEPS + s - R + 1)
                pool.sem_inc(s_begun, 1)
                pool.indirect_dma_start(got[:, u, :], None, table,
                                        bass.IndirectOffsetOnAxis(ap=idx_s[:, u:u + 1], axis=0)).then_inc(s_g[u], 16)

            for k in range(PASSES):
                pool.wait_ge(s_tst, 16 * (k + 1))
                for s in range(R):
                    gather(k, s, s)
                with pool.Fori(1, TSTEPS // R, 1) as i:
                    for u in range(R):
                        gather(k, i * R + u, u)

        @block.scalar
        def _(act):
            def std(n):
                act.wait_ge(s_var, n)
                nc.scalar.activation(rstd[:, :], rstd[:, :], ACT.Sqrt).then_inc(s_std, 1)

            std(1)
            act.wait_ge(s_w, 16 * N_WEIGHTS)

            def silu1(s, u):
                act.wait_ge(s_mm1, s + 1)
                wait(act, s_mm2, s - 1)
                nc.scalar.activation(h1[:, u, :].rearrange("p (a b) -> p a b", a=2), ps[:, 2 * u:2 * u + 2, 0:CH // 2],
                                     ACT.Silu, bias=b1s[:, 0:1]).then_inc(s_h1, 1)

            def gate(s, u):
                act.wait_ge(s_mm2, s + 1)
                wait(act, s_msg, s - 1)
                v = ps[:, 4 + u, :].rearrange("p (q d) -> p q d", q=QT)
                nc.scalar.activation(sl[:, u, :, :], v[:, :, 0:D], ACT.Silu)
                nc.scalar.activation(th[:, u, :, :], v[:, :, D:2 * D], ACT.Tanh, scale=0.5).then_inc(s_sl, 1)

            silu1(0, 0)
            for s in range(1, R0):
                silu1(s, s % 2)
                gate(s - 1, (s - 1) % 2)
            with act.Fori(1, CSTEPS // R0, 1) as i:
                for u in range(R0):
                    silu1(i * R0 + u, u % 2)
                    gate(i * R0 + u - 1, (u - 1) % 2)
            gate(CSTEPS - 1, (CSTEPS - 1) % 2)

            at_n = [0]

            def linear(k):
                for g, pairs in enumerate(GROUPS):
                    for o in range(LINEARS[k]):
                        at_n[0] += 1
                        act.wait_ge(s_tp, at_n[0])
                        n = len(pairs) * P
                        nc.scalar.activation(at[:, g % 2, o, 0:n], ps[:, 2 * (g % 2) + o, 0:n], ACT.Copy).then_inc(s_at, 1)

            def stage(k, s, u):
                w, t = window(act, swin_t if k == 1 else dwin_t, s, TSTEPS)
                wait(act, s_mm, k * TSTEPS + s - R + 1)
                of = rec[:, ds(t, 1), 1:2].rearrange("p a b -> p (a b)") if k == 1 else src_i[:, ds(t, 1)]
                nc.scalar.activation(idx_s[:, u:u + 1], of, ACT.Copy).then_inc(s_idx, 1)

            for u in range(R):
                act.wait_ge(s_sc[u], 16 * (TILES // R))
            for k in range(PASSES):
                if k < 3:
                    std(2 + 2 * k if k < 2 else 6)
                    if k < 2:
                        act.wait_ge(s_var, 3 + 2 * k)
                        sc = scale1 if k == 0 else scale2
                        nc.scalar.activation(sc[:, :], sc[:, :], ACT.Sqrt).then_inc(s_std, 1)
                if k == 0:
                    linear(0)
                if k == 1:
                    act.wait_ge(s_rec, 16)
                for s in range(R):
                    stage(k, s, s)
                with act.Fori(1, TSTEPS // R, 1) as i:
                    for u in range(R):
                        stage(k, i * R + u, u)
                if k:
                    linear(k)

        @block.tensor
        def _(pe):
            pe.wait_ge(s_const, 6)
            pe.wait_ge(s_cnt, 1)
            nc.tensor.matmul(ps[:, 0, 0:NW], before[:, :], cnt[:, 0, :], start=True, stop=False)
            nc.tensor.matmul(ps[:, 0, 0:NW], ones[:, :], cex[:, 0, :], start=False, stop=True)
            nc.tensor.matmul(ps[0:NW, 1, 0:1], cex[:, 0, :], ones[:, 0:1], start=True, stop=True)
            nc.tensor.matmul(ps[0:NW, 2, 0:1], cex[:, 1, :], ones[:, 0:1], start=True, stop=True).then_inc(s_tot, 1)
            for n, steps in enumerate((CSTEPS, TSTEPS, TSTEPS)):
                pe.wait_ge(s_wind, n + 1)
                for j in range(0, steps, 512):
                    m = min(512, steps - j)
                    last = nc.tensor.matmul(ps[0:1, 4 + j // 512, 0:m], ones[0:NW, 0:1], s2v[0:NW, TILES + j:TILES + j + m],
                                            start=True, stop=True)
                last.then_inc(s_wsum, 1)
            pe.wait_ge(s_w, 16 * N_WEIGHTS)
            pe.wait_ge(s_win, 3)

            def up(s, u):
                wait(pe, s_h1, s - 1)
                pe.wait_ge(s_xc[u], 16 * (s // R0 + 1) if isinstance(s, int) else (s - u) * (16 // R0) + 16)
                for h in range(2):
                    last = nc.tensor.matmul(ps[:, 2 * (u % 2) + h, 0:CH // 2], w1s[D * h:D * (h + 1), :],
                                            xs[D * h:D * (h + 1), u, :], start=True, stop=True)
                last.then_inc(s_mm1, 1)

            def mid(s, u):
                wait(pe, s_sl, s - 1)
                pe.wait_ge(s_h1, s + 1)
                nc.tensor.matmul(ps[:, 4 + u, :], ones[0:1, :], b2s[:, :], start=True, stop=False)
                for q in range(QT):
                    last = nc.tensor.matmul(ps[:, 4 + u, q * P:(q + 1) * P], h1[:, u, q * P:(q + 1) * P], w2s[:, :],
                                            start=False, stop=q == QT - 1)
                last.then_inc(s_mm2, 1)

            def scat(s, u):
                pe.wait_ge(s_oh0, s + 1)
                pe.wait_ge(s_msg, s + 1)
                wait(pe, s_acc, s - 1)
                for q in range(QT):
                    last = nc.tensor.matmul(ps[:, 6 + u, 0:MW], oh0[:, u, q, :], msg[:, u, q, :],
                                            start=q == 0, stop=q == QT - 1)
                last.then_inc(s_scat, 1)

            up(0, 0)
            up(1, 1)
            mid(0, 0)
            for s in (2, 3):
                up(s, s)
                mid(s - 1, (s - 1) % 2)
                scat(s - 2, s % 2)
            with pe.Fori(1, CSTEPS // R0, 1) as i:
                for u in range(R0):
                    up(i * R0 + u, u)
                    mid(i * R0 + u - 1, (u - 1) % 2)
                    scat(i * R0 + u - 2, u % 2)
            mid(CSTEPS - 1, 1)
            scat(CSTEPS - 2, 0)
            scat(CSTEPS - 1, 1)

            def degree(i, u, start, stop):
                pe.wait_ge(s_do, i + 1)
                nc.tensor.matmul(ps[:, 0, 0:NW], ohd[:, u, :], ohw[:, u, :], start=start, stop=stop,
                                 skip_group_check=True).then_inc(s_dm, 1)

            for t in range(4):
                degree(t, t, t == 0, False)
            with pe.Fori(1, TILES // 4, 1) as i:
                for u in range(4):
                    degree(i * 4 + u, u, False, u == 3)

            at_n, ev_n = [0], [0]

            def linear(k):
                ws = {0: [0], 1: [1], 2: [2, 3], 3: [4, 5]}[k]
                n_op = LINEARS[k]
                pe.wait_ge(s_op, k + 1)
                srcs = {0: [H], 1: [S1], 2: [S1, H], 3: [S1, H]}[k]

                def turn(g):
                    for o in range(n_op):
                        for j, pair in enumerate(GROUPS[g]):
                            last = nc.tensor.transpose(ps[:, 2 * (g % 2) + o, j * P:(j + 1) * P],
                                                       srcs[o][:, 2 * pair:2 * pair + 2, :].rearrange("p a b -> p (a b)"),
                                                       ident[:, :])
                        last.then_inc(s_tp, 1)

                turn(0)
                for g in range(len(GROUPS)):
                    if g + 1 < len(GROUPS):
                        turn(g + 1)
                    at_n[0] += n_op
                    pe.wait_ge(s_at, at_n[0])
                    if g >= 2:
                        pe.wait_ge(s_ev, ev_n[0] + g - 1)
                    for j in range(len(GROUPS[g])):
                        for o in range(n_op):
                            last = nc.tensor.matmul(ps[:, 4 + g % 2, j * P:(j + 1) * P], at[:, g % 2, o, j * P:(j + 1) * P],
                                                    wns[ws[o]][:, :], start=o == 0, stop=o == n_op - 1)
                    last.then_inc(s_y, 1)
                ev_n[0] += len(GROUPS)

            def add_up(k, s, u):
                pe.wait_ge(s_oh, k * TSTEPS + s + 1)
                if isinstance(s, int):
                    pe.wait_ge(s_g[u], 16 * (k * (TSTEPS // R) + s // R + 1))
                else:
                    pe.wait_ge(s_g[u], (s - u) * (16 // R) + 16 * (k * (TSTEPS // R) + 1))
                nc.tensor.matmul(ps[:, u, 0:D], oh[:, u, :], got[:, u, :], start=True, stop=True).then_inc(s_mm, 1)

            for k in range(PASSES):
                if k == 0:
                    linear(0)
                for s in range(R):
                    add_up(k, s, s)
                with pe.Fori(1, TSTEPS // R, 1) as i:
                    for u in range(R):
                        add_up(k, i * R + u, u)
                if k:
                    linear(k)

        @block.vector
        def _(dve):
            chain = [0]

            def link(ins):
                chain[0] += 1
                ins.then_inc(s_v, 1)
                dve.wait_ge(s_v, chain[0])

            V = nc.vector
            dve.wait_ge(s_const, 6)
            dve.wait_ge(s_rows, 48)
            link(V.tensor_single_scalar(tmp_i, srow_i, 7, op=ALU.logical_shift_right))
            link(V.tensor_copy(hi_f[:, :], tmp_i))
            link(V.tensor_single_scalar(tmp_i, srow_i, P - 1, op=ALU.bitwise_and))
            link(V.tensor_copy(lo_f[:, :], tmp_i))
            link(V.memset(recf[:, :, 3:4], 0.0))
            V.tensor_copy(rec[:, :, 0:1].rearrange("p t a -> p (t a)"), srow_i)
            V.tensor_copy(rec[:, :, 1:2].rearrange("p t a -> p (t a)"), drow_i)
            link(V.tensor_copy(recf[:, :, 2:3].rearrange("p t a -> p (t a)"), wrow))
            dve.wait_ge(s_dt, 16)
            link(V.tensor_copy(dst_f[:, :], dtile_i[:, :]))
            link(V.tensor_single_scalar(tmp_i, drow_i, 7, op=ALU.logical_shift_right))
            link(V.tensor_copy(pos, tmp_i))

            for n, key in enumerate((hi_f[:, :], pos)):
                with dve.Fori(0, NW, 1) as w:
                    V.tensor_scalar(mask, key, wcol[:, ds(w, 1)], None, ALU.is_equal, ALU.add,
                                    accum_out=cnt[:, n, ds(w, 1)]).then_inc(s_v, 1)
                    dve.wait_ge(s_v, w + chain[0] + 1)
                chain[0] += NW
                link(V.memset(cex[:, n, 0:1], 0.0))
                link(V.tensor_tensor_scan(cex[:, n, 1:NW], ones[:, 0:NW - 1], cnt[:, n, 0:NW - 1], 0.0, ALU.mult, ALU.add))
            V.memset(msg[:, :, :, D:MW], 1.0).then_inc(s_cnt, 1)
            dve.wait_ge(s_tot, 1)
            link(V.tensor_copy(base[:, :], ps[:, 0, 0:NW]))
            for n, (bank, shift, last) in enumerate(((2, 9, CHUNKS - 1), (2, 7, TILES - 1), (1, 7, TILES - 1))):
                link(V.tensor_copy(wst_i[:, 0:1], ps[0:NW, bank, 0:1]))
                link(V.tensor_single_scalar(wst_i[:, 1:2], wst_i[:, 0:1], shift, op=ALU.logical_shift_right))
                link(V.tensor_copy(wst[:, 0:1], wst_i[:, 1:2]))
                link(V.tensor_scalar(wst[:, 1:2], wst[:, 0:1], float(last), pidx[0:NW, :], ALU.min, ALU.add))
                steps = CSTEPS if n == 0 else TSTEPS
                V.tensor_scalar(s2v[0:NW, TILES:TILES + steps] if steps <= TILES else s2v[0:NW, TILES:TILES + steps],
                                iota_all[0:NW, 0:steps], wst[:, 1:2], None, ALU.is_ge).then_inc(s_wind, 1)
                dve.wait_ge(s_wsum, n + 1)
                tab = (dwin_c, dwin_t, swin_t)[n]
                for j in range(0, steps, 512):
                    m = min(512, steps - j)
                    ins = V.tensor_single_scalar(tab[:, j:j + m], ps[0:1, 4 + j // 512, 0:m], -1.0, op=ALU.add)
                ins.then_inc(s_win, 1)
                dve.wait_ge(s_win, n + 1)
            with dve.Fori(0, NW, 1) as w:
                n0 = chain[0]
                V.tensor_scalar(mask, hi_f[:, :], wcol[:, ds(w, 1)], None, ALU.is_equal).then_inc(s_v, 1)
                dve.wait_ge(s_v, w * 3 + n0 + 1)
                V.tensor_tensor_scan(run, ones[:, 0:1].broadcast_to([P, TILES]), mask, base[:, ds(w, 1)], ALU.mult, ALU.add).then_inc(s_v, 1)
                dve.wait_ge(s_v, w * 3 + n0 + 2)
                dve.sem_inc(s_placed, 1)
                V.copy_predicated(pos, mask.bitcast(i32), run).then_inc(s_v, 1)
                dve.wait_ge(s_v, w * 3 + n0 + 3)
            chain[0] += 3 * NW
            link(V.tensor_scalar(tmp_i, pos, -1.0, None, ALU.add))
            link(V.tensor_single_scalar(slot_i[:, :], tmp_i, P - 1, op=ALU.bitwise_and))
            link(V.tensor_single_scalar(srow_i, tmp_i, 7, op=ALU.logical_shift_right))
            V.scalar_tensor_tensor(out=slot_i[:, :], in0=slot_i[:, :], scalar=float(TILES), in1=srow_i,
                                   op0=ALU.mult, op1=ALU.add).then_inc(s_slot, 1)
            dve.wait_ge(s_slot, 1)

            var_n = [0]
            bc = lambda t: t[:, :].rearrange("p (w a) -> p w a", a=1).broadcast_to([P, NWP, D])

            def layernorm():
                link(V.tensor_reduce(mean[:, :], X[:, :, :], axis=AX.X, op=ALU.add))
                link(V.tensor_single_scalar(mean[:, :], mean[:, :], 1.0 / D, op=ALU.mult))
                link(V.tensor_tensor(H[:, :, :], X[:, :, :], bc(mean), ALU.subtract))
                link(V.tensor_tensor(S2[:, :, :], H[:, :, :], H[:, :, :], ALU.mult))
                link(V.tensor_reduce(rstd[:, :], S2[:, :, :], axis=AX.X, op=ALU.add))
                V.tensor_scalar(rstd[:, :], rstd[:, :], 1.0 / D, EPS, ALU.mult, ALU.add).then_inc(s_var, 1)
                var_n[0] += 1
                dve.wait_ge(s_std, var_n[0])
                link(V.reciprocal(rstd[:, :], rstd[:, :]))
                link(V.scalar_tensor_tensor(out=H[:, :, :], in0=H[:, :, :], scalar=0.0, in1=bc(rstd),
                                            op0=ALU.max, op1=ALU.mult))

            dve.wait_ge(s_x, 16)
            layernorm()
            link(V.memset(ACC[:, :, :], 0.0))

            def onehots(s, u):
                w, c = window(dve, dwin_c, s, CSTEPS)
                wait(dve, s_scat, s - 1)
                for q in range(QT):
                    ins = V.tensor_scalar(oh0[:, u, q, :], iota_all[:, ds(w * P, P)], dst_f[:, ds(c * QT + q, 1)], None,
                                          ALU.is_equal)
                ins.then_inc(s_oh0, 1)

            def message(s, u):
                dve.wait_ge(s_sl, s + 1)
                wait(dve, s_scat, s - 1)
                V.scalar_tensor_tensor(out=msg[:, u, :, 0:D], in0=th[:, u, :, :], scalar=1.0, in1=sl[:, u, :, :],
                                       op0=ALU.add, op1=ALU.mult).then_inc(s_msg, 1)

            def add_chunk(s, u):
                w = window_of(dve, dwin_c, s)
                dve.wait_ge(s_scat, s + 1)
                wait(dve, s_acc, s)
                to = accv[:, ds(w * MW, MW)]
                V.tensor_tensor(to, to, ps[:, 6 + u, 0:MW], ALU.add).then_inc(s_acc, 1)

            onehots(0, 0)
            onehots(1, 1)
            message(0, 0)
            for s in (2, 3):
                add_chunk(s - 2, s % 2)
                onehots(s, s % 2)
                message(s - 1, (s - 1) % 2)
            with dve.Fori(1, CSTEPS // R0, 1) as i:
                for u in range(R0):
                    add_chunk(i * R0 + u - 2, u % 2)
                    onehots(i * R0 + u, u % 2)
                    message(i * R0 + u - 1, (u - 1) % 2)
            add_chunk(CSTEPS - 2, 0)
            message(CSTEPS - 1, 1)
            add_chunk(CSTEPS - 1, 1)

            def degree(i, u):
                wait(dve, s_dm, i - 3)
                V.tensor_scalar(ohd[:, u, :], iota_all[:, 0:P], lo_f[:, ds(i, 1)], None, ALU.is_equal)
                V.tensor_scalar(ohw[:, u, :], wcol[:, :], hi_f[:, ds(i, 1)],
                                recf[:, ds(i, 1), 2:3].rearrange("p a b -> p (a b)"),
                                ALU.is_equal, ALU.mult).then_inc(s_do, 1)

            for t in range(4):
                degree(t, t)
            with dve.Fori(1, TILES // 4, 1) as i:
                for u in range(4):
                    degree(i * 4 + u, u)
            dve.wait_ge(s_dm, TILES)
            link(V.memset(scale2[:, :], 1.0))
            link(V.tensor_scalar(scale2[:, 0:NW], ps[:, 0, 0:NW], 1.0, None, ALU.add))

            dve.wait_ge(s_acc, CSTEPS)
            link(V.tensor_copy(count[:, :], ACC[:, :, D]))
            link(V.tensor_tensor(X[:, :, :], X[:, :, :], H[:, :, :], ALU.add))
            link(V.scalar_tensor_tensor(out=X[:, :, :], in0=ACC[:, :, 0:D], scalar=0.5, in1=X[:, :, :],
                                        op0=ALU.mult, op1=ALU.add))
            layernorm()

            y_n = [0]

            def products(evac):
                for g, pairs in enumerate(GROUPS):
                    y_n[0] += 1
                    dve.wait_ge(s_y, y_n[0])
                    w0, nw = 2 * pairs[0], 2 * len(pairs)
                    yv = ps[:, 4 + g % 2, 0:nw * D].rearrange("p (w d) -> p w d", d=D)
                    evac(slice(w0, w0 + nw), nw, yv).then_inc(s_ev, 1)
                dve.wait_ge(s_ev, y_n[0])

            def degrees(sc, deg):
                link(V.tensor_scalar(mean[:, :], deg, 0.0, None, ALU.is_gt))
                link(V.tensor_tensor(sc[:, :], deg, mean[:, :], ALU.mult))
                link(V.scalar_tensor_tensor(out=sc[:, :], in0=mean[:, :], scalar=-1.0, in1=sc[:, :],
                                            op0=ALU.mult, op1=ALU.add))
                V.tensor_scalar(sc[:, :], sc[:, :], 1.0, None, ALU.add).then_inc(s_var, 1)
                var_n[0] += 1
                dve.wait_ge(s_std, var_n[0])
                link(V.reciprocal(sc[:, :], sc[:, :]))
                link(V.tensor_tensor(sc[:, :], sc[:, :], mean[:, :], ALU.mult))

            bias = lambda b, nw: b[:, :].rearrange("p (a d) -> p a d", a=1).broadcast_to([P, nw, D])

            def spread(k):
                off = k * TSTEPS
                tab = swin_t if k == 1 else dwin_t
                key = srt_f if k == 1 else dst_f

                def onehot(s, u):
                    w, t = window(dve, tab, s, TSTEPS)
                    if k == 1:
                        V.tensor_scalar(oh[:, u, :], iota_all[:, ds(w * P, P)], key[:, ds(t, 1)],
                                        recf[:, ds(t, 1), 2:3].rearrange("p a b -> p (a b)"),
                                        ALU.is_equal, ALU.mult).then_inc(s_oh, 1)
                    else:
                        V.tensor_scalar(oh[:, u, :], iota_all[:, ds(w * P, P)], key[:, ds(t, 1)], None,
                                        ALU.is_equal).then_inc(s_oh, 1)

                def add(s, u):
                    w = window_of(dve, tab, s)
                    dve.wait_ge(s_mm, off + s + 1)
                    wait(dve, s_add, off + s)
                    to = ACC[:, ds(w, 1), 0:D].rearrange("p a b -> p (a b)")
                    V.tensor_tensor(to, to, ps[:, u, 0:D], ALU.add).then_inc(s_add, 1)

                for s in range(R):
                    onehot(s, s)
                with dve.Fori(1, TSTEPS // R, 1) as i:
                    for u in range(R):
                        add(i * R + u - R, u)
                        onehot(i * R + u, u)
                for s in range(TSTEPS - R, TSTEPS):
                    add(s, s % R)
                dve.wait_ge(s_add, off + TSTEPS)

            link(V.tensor_scalar(scale3[:, :], count[:, :], 1.0, None, ALU.add))
            degrees(scale1, scale3[:, :])
            V.memset(scale3[:, 0:1], 0.0).then_inc(s_op, 1)
            sc1 = lambda ww, nw: scale1[:, ww].rearrange("p (w a) -> p w a", a=1).broadcast_to([P, nw, D])
            products(lambda ww, nw, y: V.tensor_tensor(S1[:, ww, :], y, sc1(ww, nw), ALU.mult))
            V.tensor_copy(ACC[:, :, 0:D], S1[:, :, :]).then_inc(s_tab, 1)
            spread(0)
            link(V.tensor_tensor(S1[:, :, :], ACC[:, :, 0:D], bc(scale1), ALU.mult))
            link(V.tensor_tensor(S1[:, :, :], S1[:, :, :], bias(bns[0], NWP), ALU.add))
            link(V.scalar_tensor_tensor(out=X[:, :, :], in0=S1[:, :, :], scalar=0.0, in1=X[:, :, :],
                                        op0=ALU.max, op1=ALU.add))
            layernorm()
            link(V.tensor_copy(scale3[:, :], scale2[:, :]))
            degrees(scale2, scale3[:, :])
            dve.wait_ge(s_rec, 16)
            link(V.tensor_copy(srt_f[:, :], rec[:, :, 0:1].rearrange("p t a -> p (t a)")))
            link(V.tensor_tensor(S1[:, :, :], H[:, :, :], bc(scale2), ALU.mult))
            V.tensor_copy(ACC[:, :, 0:D], S1[:, :, :]).then_inc(s_tab, 1)
            spread(1)
            V.tensor_tensor(S1[:, :, :], ACC[:, :, 0:D], bc(scale2), ALU.mult).then_inc(s_op, 1)
            dve.wait_ge(s_op, 2)
            link(V.tensor_tensor(X[:, :, :], X[:, :, :], bias(bns[1], NWP), ALU.add))
            products(lambda ww, nw, y: V.tensor_tensor(X[:, ww, :], X[:, ww, :], y, ALU.add))
            layernorm()
            link(V.tensor_scalar(scale3[:, :], count[:, :], 1.0, None, ALU.max))
            link(V.reciprocal(scale3[:, :], scale3[:, :]))
            V.memset(ACC[:, :, :], 0.0).then_inc(s_tab, 1)
            dve.wait_ge(s_tab, 3)
            spread(2)
            V.tensor_tensor(S1[:, :, :], ACC[:, :, 0:D], bc(scale3), ALU.mult).then_inc(s_op, 1)
            products(lambda ww, nw, y: V.tensor_tensor(S2[:, ww, :], y, bias(bns[2], nw), ALU.add))
            link(V.tensor_scalar(H[:, :, :], S2[:, :, :], 0.0, None, ALU.max))
            V.memset(ACC[:, :, :], 0.0).then_inc(s_tab, 1)
            dve.wait_ge(s_tab, 4)
            spread(3)
            V.tensor_tensor(S1[:, :, :], ACC[:, :, 0:D], bc(scale3), ALU.mult).then_inc(s_op, 1)
            link(V.tensor_tensor(X[:, :, :], X[:, :, :], bias(bns[3], NWP), ALU.add))
            products(lambda ww, nw, y: V.tensor_tensor(X[:, ww, :], X[:, ww, :], y, ALU.add))
            V.memset(mean[:, 0:1], 0.0).then_inc(s_fin, 1)


def kernel(**inputs):
    import numpy as np
    import concourse.bacc as bacc
    from concourse.bass_utils import run_bass_kernel_spmd as run

    def a(name):
        return np.ascontiguousarray(inputs[name])

    def padded(v, fill):
        return np.concatenate([v, np.full((EDGES - N_EDGES,), fill, v.dtype)])

    def twice(w):
        both = np.zeros((P, P), w.dtype)
        both[0:D, 0:D] = w
        both[D:P, D:P] = w
        return both

    def rows(b):
        return np.ascontiguousarray(np.broadcast_to(b, (P, D)))

    x = np.zeros((NWP * P, D), np.float32)
    x[0:N_NODES] = a("x")
    e = np.zeros((EDGES, D), np.float32)
    e[0:N_EDGES] = a("edge_attr_64")
    src, dst = padded(a("src"), DUMMY), padded(a("dst"), DUMMY)
    w = padded(a("edge_weight"), 0)
    w2g2 = np.zeros((P, P), np.float32)
    w2g2[0:D, 0:D] = a("L0_gnn_W2")
    w2g2[D:P, D:P] = a("L0_gnn_G2")
    w1g1 = np.concatenate([a("L0_gnn_W1"), a("L0_gnn_G1")], axis=1)
    arrays = {
        "x": x.reshape(NWP, P, D).transpose(1, 0, 2),
        "edge_t": e.reshape(CHUNKS, 2, CH // 2, D).transpose(0, 1, 3, 2).reshape(CHUNKS, P, CH // 2),
        "dst_tiles": dst.reshape(TILES, P).T, "src_tiles": src.reshape(TILES, P).T,
        "src_rows": src.reshape(P, TILES), "dst_rows": dst.reshape(P, TILES), "w_rows": w.reshape(P, TILES),
        "w1g1": np.concatenate([w1g1, w1g1], axis=0), "w2g2": w2g2,
        "b1g1": np.concatenate([a("L0_gnn_b1"), a("L0_gnn_g1")]).reshape(P, 1),
        "b2g2": np.tile(np.concatenate([a("L0_gnn_b2"), a("L0_gnn_g2")]), QT).reshape(1, CH),
        "w_gcn": twice(a("L1_gnn_W")), "w_l2": twice(a("L2_gnn_W").T),
        "w_l0": twice(a("L3_gnn_Wl0")), "w_r0": twice(a("L3_gnn_Wr0")),
        "w_l1": twice(a("L3_gnn_Wl1")), "w_r1": twice(a("L3_gnn_Wr1")),
        "b_gcn": rows(a("L1_gnn_b")), "b_l2": rows(a("L2_gnn_b")),
        "b_l0": rows(a("L3_gnn_bl0")), "b_l1": rows(a("L3_gnn_bl1")),
    }
    nc = bacc.Bacc("TRN2", target_bir_lowering=False, num_devices=1)
    sent, args = {}, []
    for name, v in arrays.items():
        sent[f"in_{name}"] = np.ascontiguousarray(v)
        args.append(nc.dram_tensor(f"in_{name}", v.shape, mybir.dt.from_np(v.dtype), kind="ExternalInput").ap())
    args.append(nc.dram_tensor("out_0", (N_NODES, D), mybir.dt.float32, kind="ExternalOutput").ap())
    gnn_kernel(nc, *args)
    return run(nc, [sent], core_ids=[0]).results[0]["out_0"]
```

```python
import concourse.bass as bass
from concourse import mybir
from contextlib import ExitStack

P = 128
N_NODES, N_EDGES, D = 6250, 200000, 64
NW = -(-N_NODES // P)
NWP = NW + NW % 2
NODES = NW * P
DUMMY = NODES - 1
CH = 512
R = 8
EDGES = -(-N_EDGES // (R * P)) * R * P
TILES = EDGES // P
CHUNKS = EDGES // CH
QT = CH // P
CSTEPS = CHUNKS + NW - 1
TSTEPS = TILES + NW - 1
R0 = 4
TURNS = TSTEPS // R
DEGREE_TURNS = TILES // R
WIDE = 3328
MW = D + 1
EPS = 1e-5


def ds(start, size):
    return bass.DynSlice(start, size)


def wait(eng, sem, value):
    if not isinstance(value, int) or value > 0:
        eng.wait_ge(sem, value)


def gnn_kernel(nc, x, edge_t, dst_tiles, src_tiles, src_rows, dst_rows, w_rows, w1g1, w2g2, b1g1, b2g2,
               w_gcn, w_l2, w_l0, w_r0, w_l1, w_r1, b_gcn, b_l2, b_l0, b_l1, out):
    f32, bf16, i32 = mybir.dt.float32, mybir.dt.bfloat16, mybir.dt.int32
    ALU, ACT, AX = mybir.AluOpType, mybir.ActivationFunctionType, mybir.AxisListType
    ctx = ExitStack()
    with ctx:
        def sb(name, shape, dt=f32):
            return ctx.enter_context(nc.sbuf_tensor(name, shape, dt))

        def sem(name):
            return ctx.enter_context(nc.semaphore(name))

        records = nc.dram_tensor("records", (EDGES, 4), i32).ap()
        table = nc.dram_tensor("table", (NODES, D), f32).ap()

        X = sb("X", [P, NWP, D])
        H = sb("H", [P, NWP, D])
        ACC = sb("ACC", [P, NWP, MW])
        s1v = sb("S1", [P, WIDE])
        s2v = sb("S2", [P, WIDE])
        S1 = s1v[:, 0:NWP * D].rearrange("p (a b) -> p a b", b=D)
        S2 = s2v[:, 0:NWP * D].rearrange("p (a b) -> p a b", b=D)
        count = sb("count", [P, NWP])
        scale1 = sb("scale1", [P, NWP])
        scale2 = sb("scale2", [P, NWP])
        scale3 = sb("scale3", [P, NWP])
        mean = sb("mean", [P, NWP])
        rstd = sb("rstd", [P, NWP])
        iota = sb("iota", [P, TSTEPS])
        dkey_c = sb("dkey_c", [P, CSTEPS * QT])
        dkey = sb("dkey", [P, TSTEPS])
        dget = sb("dget", [P, TSTEPS], i32)
        rec = sb("rec", [P, TILES, 4], i32)
        recf = rec[:, :, :].bitcast(f32)
        skey = sb("skey", [P, TSTEPS])
        sget = sb("sget", [P, TSTEPS], i32)
        swgt = sb("swgt", [P, TSTEPS])
        hi_f = sb("hi_f", [P, TILES])
        lo_f = sb("lo_f", [P, TILES])
        slot_i = sb("slot_i", [P, TILES], i32)
        accv = ACC[:, :, :].rearrange("p a b -> p (a b)")
        srow_i = s1v[:, 0:TILES].bitcast(i32)
        drow_i = s1v[:, TILES:2 * TILES].bitcast(i32)
        wrow = s2v[:, 0:TILES]
        mask = s2v[:, TILES:2 * TILES]
        run = skey[:, 0:TILES]
        pos = accv[:, 0:TILES]
        tmp_i = accv[:, TILES:2 * TILES].bitcast(i32)
        dtile_i = swgt[:, 0:TILES].bitcast(i32)
        stile_i = sget[:, 0:TILES]
        ident = sb("ident", [P, P])
        before = sb("before", [P, P])
        ones = sb("ones", [P, P])
        wcol = sb("wcol", [P, NW])
        wfirst = sb("wfirst", [P, NW])
        pidx = sb("pidx", [P, 1])
        cnt = sb("cnt", [P, 2, NW])
        cex = sb("cex", [P, 2, NW])
        base = sb("base", [P, NW])
        wst_i = sb("wst_i", [NW, 4], i32)
        wst = sb("wst", [NW, 4])
        wbeg = [sb(f"wbeg{i}", [1, NW], i32) for i in range(3)]
        dwin_c = sb("dwin_c", [1, CSTEPS], i32)
        dwin_t = sb("dwin_t", [1, TSTEPS], i32)
        swin_t = sb("swin_t", [1, TSTEPS], i32)
        w1s = sb("w1s", [P, 2, P])
        w2s = sb("w2s", [P, P])
        b1s = sb("b1s", [P, 1])
        b2s = H[:, 0:CH // D, :].rearrange("p a b -> p (a b)")
        b2t = H[:, CH // D:2 * CH // D, :].rearrange("p a b -> p (a b)")
        b2u = H[:, 2 * CH // D:3 * CH // D, :].rearrange("p a b -> p (a b)")
        b2b = sb("b2b", [P, CH], bf16)
        onesb = sb("onesb", [P, P], bf16)
        part = sb("part", [P, 3])
        wns = [sb(f"wn{i}", [P, P]) for i in range(6)]
        bns = [sb(f"bn{i}", [P, D]) for i in range(4)]
        ring = sb("ring", [P, R0 * CH])
        xs = ring[:, 0:2 * CH].rearrange("p (r e) -> p r e", r=R0)
        h1 = ring[:, 2 * CH:4 * CH].rearrange("p (r e) -> p r e", r=2)
        at = ring[:, :].rearrange("p (a b e) -> p a b e", a=2, b=2)
        mlp = sb("mlp", [P, 2 * QT * (2 * D + MW)])
        quarters = lambda at, n: mlp[:, at * 2 * QT:(at + n) * 2 * QT].rearrange("p (a q d) -> p a q d", a=2, q=QT)
        sl, th, msg = quarters(0, D), quarters(D, D), quarters(2 * D, MW)
        ohd = mlp[:, 0:R * P].rearrange("p (r n) -> p r n", r=R)
        wgt = dkey_c[:, 0:TILES]
        idx_s = sb("idx_s", [P, 2, R], i32)
        rec_s = sb("rec_s", [P, 2, R, 4], i32)
        got = sb("got", [P, 2, R, D])
        oh = sb("oh", [P, 2, R, P])
        oh0 = oh[:, 0, :, :].rearrange("p (a q) n -> p a q n", q=QT)
        ohw = sb("ohw", [P, R, NW])
        ps = ctx.enter_context(nc.psum_tensor("ps", [P, 8, 512], f32))

        s_w, s_x, s_dt, s_st, s_rows = sem("s_w"), sem("s_x"), sem("s_dt"), sem("s_st"), sem("s_rows")
        s_const, s_pc = sem("s_const"), sem("s_pc")
        s_v = sem("s_v")
        s_cnt, s_tot, s_wst, s_wind, s_wsum, s_win = (sem(n) for n in ("s_cnt", "s_tot", "s_wst", "s_wind", "s_wsum", "s_win"))
        s_slot, s_stg, s_sc = sem("s_slot"), sem("s_stg"), [sem(f"s_sc{i}") for i in range(2)]
        s_xc = [sem(f"s_xc{i}") for i in range(R0)]
        s_mm1, s_h1, s_mm2, s_sl, s_msg, s_oh0, s_scat, s_acc = (sem(n) for n in (
            "s_mm1", "s_h1", "s_mm2", "s_sl", "s_msg", "s_oh0", "s_scat", "s_acc"))
        s_dp, s_do, s_dm = sem("s_dp"), sem("s_do"), sem("s_dm")
        s_rec = sem("s_rec")
        s_idx, s_g = ([sem(f"{n}{i}") for i in range(2)] for n in ("s_idx", "s_g"))
        s_oh, s_mm, s_add = sem("s_oh"), sem("s_mm"), [sem(f"s_add{i}") for i in range(R)]
        s_wt = sem("s_wt")
        s_key, s_lay, s_lay2, s_kept = sem("s_key"), sem("s_lay"), sem("s_lay2"), sem("s_kept")
        s_begun, s_placed = sem("s_begun"), sem("s_placed")
        s_var, s_std = sem("s_var"), sem("s_std")
        s_op, s_tp, s_at, s_y, s_ev = sem("s_op"), sem("s_tp"), sem("s_at"), sem("s_y"), sem("s_ev")
        s_tab, s_tst, s_fin, s_out = sem("s_tab"), sem("s_tst"), sem("s_fin"), sem("s_out")
        block = ctx.enter_context(nc.Block())

        N_WEIGHTS = 4 + 6 + 4
        PASSES = 4
        GROUPS = [list(range(g, min(g + 4, NWP // 2))) for g in range(0, NWP // 2, 4)]
        LINEARS = [1, 1, 2, 2]

        def load(eng, ap, top):
            _, values = nc.values_load_multi_w_load_instructions(
                ap, engines=[eng.engine], min_val=0, max_val=top,
                skip_runtime_bounds_check_because="counts of windows that have begun, the first of which always has, and steps at which they begin")
            return values

        def windows(eng, tab, s, n):
            return load(eng, tab[0:1, ds(s, n)], NW - 1)

        def less(a, b, top):
            return nc.s_assert_within(a - b, 0, top, skip_runtime_bounds_check_because="each step goes to a window or to a tile, and window w begins w steps or more after the first")

        @block.sync
        def _(sp):
            sp.dma_start(srow_i, src_rows).then_inc(s_rows, 16)
            sp.dma_start(drow_i, dst_rows).then_inc(s_rows, 16)
            sp.dma_start(wrow, w_rows).then_inc(s_rows, 16)
            sp.dma_start(X[:, :, :], x).then_inc(s_x, 16)
            sp.dma_start(dtile_i, dst_tiles).then_inc(s_dt, 16)
            sp.dma_start(stile_i, src_tiles).then_inc(s_st, 16)
            sp.dma_start(w1s[:, :, :], w1g1.rearrange("p (h n) -> p h n", h=2)).then_inc(s_w, 16)
            sp.dma_start(b2s, b2g2).then_inc(s_w, 16)
            for to, of in [(w2s, w2g2), (b1s, b1g1)] + list(
                    zip(wns, (w_gcn, w_l2, w_l0, w_r0, w_l1, w_r1))) + list(zip(bns, (b_gcn, b_l2, b_l0, b_l1))):
                sp.dma_start(to[:, :], of).then_inc(s_w, 16)
            sp.wait_ge(s_win, 1)

            def chunk(s, u, w):
                c = less(s, w, CHUNKS - 1)
                wait(sp, s_mm1, s - R0 + 1)
                sp.dma_start(xs[:, u, :], edge_t[ds(c, 1), :, :].rearrange("a p e -> (a p) e")).then_inc(s_xc[u], 16)

            for s, w in enumerate(windows(sp, dwin_c, 0, R0)):
                chunk(s, s, w)
            with sp.Fori(1, CSTEPS // R0, 1) as i:
                for u, w in enumerate(windows(sp, dwin_c, i * R0, R0)):
                    chunk(i * R0 + u, u, w)
            for p in range(2):
                sp.wait_ge(s_sc[p], 16 * R * (TILES // R // 2))
            sp.wait_ge(s_kept, 1)
            sp.dma_start(rec[:, :, :], records.rearrange("(p t) k -> p t k", p=P)).then_inc(s_rec, 16)
            for k in range(PASSES):
                sp.wait_ge(s_tab, k + 1)
                of = [S1, S1, H, H][k]
                sp.dma_start(table.rearrange("(w p) f -> p w f", p=P), of[:, 0:NW, :]).then_inc(s_tst, 16)
                rows = sget if k == 1 else dget

                def stage(i, p):
                    wait(sp, s_mm, k * TURNS + i * 2 + p - 1)
                    sp.dma_start(idx_s[:, p, :], rows[:, ds((i * 2 + p) * R, R)]).then_inc(s_idx[p], 16)

                for p in range(2):
                    stage(0, p)
                with sp.Fori(1, TURNS // 2, 1) as i:
                    for p in range(2):
                        stage(i, p)
            sp.wait_ge(s_fin, 1)
            full = N_NODES // P
            sp.dma_start(out[0:full * P, :].rearrange("(w p) f -> p w f", p=P), X[:, 0:full, :]).then_inc(s_out, 16)
            sp.dma_start(out[full * P:N_NODES, :], X[0:N_NODES - full * P, full, :]).then_inc(s_out, 16)
            sp.wait_ge(s_out, 32)

        @block.gpsimd
        def _(pool):
            nc.gpsimd.iota(iota[:, :], [[1, TSTEPS]], base=0, channel_multiplier=0,
                           allow_small_or_imprecise_dtypes=True).then_inc(s_const, 1)
            nc.gpsimd.iota(wcol[:, :], [[1, NW]], base=0, channel_multiplier=0,
                           allow_small_or_imprecise_dtypes=True).then_inc(s_const, 1)
            nc.gpsimd.iota(pidx[:, :], [[0, 1]], base=0, channel_multiplier=1,
                           allow_small_or_imprecise_dtypes=True).then_inc(s_const, 1)
            nc.gpsimd.memset(ones[:, :], 1.0).then_inc(s_const, 1)
            nc.gpsimd.memset(ident[:, :], 0.0).then_inc(s_pc, 1)
            nc.gpsimd.memset(before[:, :], 1.0).then_inc(s_pc, 1)
            pool.wait_ge(s_pc, 2)
            nc.gpsimd.affine_select(out=ident[:, :], in_=ident[:, :], compare_op=ALU.not_equal, fill=1.0,
                                    base=0, pattern=[[-1, P]], channel_multiplier=1).then_inc(s_const, 1)
            nc.gpsimd.affine_select(out=before[:, :], in_=before[:, :], compare_op=ALU.is_gt, fill=0.0,
                                    base=0, pattern=[[1, P]], channel_multiplier=-1).then_inc(s_const, 1)
            pool.wait_ge(s_slot, 1)


            def scatter(i, p):
                t = i * 2 + p
                if not isinstance(i, int):
                    pool.wait_ge(s_sc[p], i * (16 * R))
                nc.gpsimd.tensor_copy(idx_s[:, p, :], slot_i[:, ds(t * R, R)]).then_inc(s_stg, 1)
                nc.gpsimd.tensor_copy(rec_s[:, p, :, :], rec[:, ds(t * R, R), :]).then_inc(s_stg, 1)
                pool.wait_ge(s_stg, t * 2 + 2)
                pool.sem_inc(s_begun, 1)
                for u in range(R):
                    pool.indirect_dma_start(records, bass.IndirectOffsetOnAxis(ap=idx_s[:, p, u:u + 1], axis=0),
                                            rec_s[:, p, u, :], None).then_inc(s_sc[p], 16)

            scatter(0, 0)
            scatter(0, 1)
            with pool.Fori(1, TILES // R // 2, 1) as i:
                scatter(i, 0)
                scatter(i, 1)

            def gather(k, i, p):
                pool.wait_ge(s_idx[p], (i + (k * (TURNS // 2) + 1)) * 16)
                pool.sem_inc(s_begun, 1)
                for u in range(R):
                    pool.indirect_dma_start(got[:, p, u, :], None, table,
                                            bass.IndirectOffsetOnAxis(ap=idx_s[:, p, u:u + 1], axis=0)).then_inc(s_g[p], 16)

            for k in range(PASSES):
                pool.wait_ge(s_tst, 16 * (k + 1))
                for p in range(2):
                    gather(k, 0, p)
                with pool.Fori(1, TURNS // 2, 1) as i:
                    for p in range(2):
                        gather(k, i, p)

        @block.scalar
        def _(act):
            def std(n):
                act.wait_ge(s_var, n)
                nc.scalar.activation(rstd[:, :], rstd[:, :], ACT.Sqrt).then_inc(s_std, 1)

            std(1)
            act.wait_ge(s_w, 16 * N_WEIGHTS)

            def silu1(s, u):
                act.wait_ge(s_mm1, s + 1)
                wait(act, s_mm2, s - 1)
                nc.scalar.activation(h1[:, u, :].rearrange("p (a b) -> p a b", a=2), ps[:, 2 * u:2 * u + 2, 0:CH // 2],
                                     ACT.Silu, bias=b1s[:, 0:1]).then_inc(s_h1, 1)

            def gate(s, u):
                act.wait_ge(s_mm2, s + 1)
                wait(act, s_msg, s - 1)
                v = ps[:, 4 + u, :].rearrange("p (q d) -> p q d", q=QT)
                nc.scalar.activation(sl[:, u, :, :], v[:, :, 0:D], ACT.Silu)
                nc.scalar.activation(th[:, u, :, :], v[:, :, D:2 * D], ACT.Tanh, scale=0.5).then_inc(s_sl, 1)

            silu1(0, 0)
            for s in range(1, R0):
                silu1(s, s % 2)
                gate(s - 1, (s - 1) % 2)
            with act.Fori(1, CSTEPS // R0, 1) as i:
                for u in range(R0):
                    silu1(i * R0 + u, u % 2)
                    gate(i * R0 + u - 1, (u - 1) % 2)
            gate(CSTEPS - 1, (CSTEPS - 1) % 2)

            at_n = [0]

            def linear(k):
                for g, pairs in enumerate(GROUPS):
                    for o in range(LINEARS[k]):
                        at_n[0] += 1
                        act.wait_ge(s_tp, at_n[0])
                        n = len(pairs) * P
                        nc.scalar.activation(at[:, g % 2, o, 0:n], ps[:, 2 * (g % 2) + o, 0:n], ACT.Copy).then_inc(s_at, 1)

            lay_n = [0]

            def relay(to, of, key):
                def linked(ins):
                    lay_n[0] += 1
                    ins.then_inc(s_lay, 1)
                    act.wait_ge(s_lay, lay_n[0])

                linked(nc.scalar.activation(s2v[:, 0:TILES], of, ACT.Copy))
                with act.Fori(0, NW, 1) as w:
                    s = load(act, wbeg[2][0:1, ds(w, 1)], TSTEPS - 1)[0]
                    src_at = s2v[:, ds(less(s, w, TILES - 1), TILES)]
                    if key:
                        ins = nc.scalar.activation(s1v[:, ds(s, TILES)], src_at, ACT.Identity, bias=wfirst[:, ds(w, 1)])
                    else:
                        ins = nc.scalar.activation(s1v[:, ds(s, TILES)], src_at, ACT.Copy)
                    ins.then_inc(s_lay, 1)
                    act.wait_ge(s_lay, w + (lay_n[0] + 1))
                lay_n[0] += NW
                linked(nc.scalar.activation(to, s1v[:, 0:TSTEPS], ACT.Copy))

            for k in range(PASSES):
                if k < 3:
                    std(2 + 2 * k if k < 2 else 6)
                    if k < 2:
                        act.wait_ge(s_var, 3 + 2 * k)
                        sc = scale1 if k == 0 else scale2
                        nc.scalar.activation(sc[:, :], sc[:, :], ACT.Sqrt).then_inc(s_std, 1)
                if k == 0:
                    linear(0)
                    act.wait_ge(s_rec, 16)
                    act.wait_ge(s_tst, 16)
                    act.wait_ge(s_tab, 1)
                    flat = lambda v: v.rearrange("p t a -> p (t a)")
                    relay(skey[:, :], flat(rec[:, :, 0:1]), True)
                    relay(sget[:, :], flat(rec[:, :, 1:2]), False)
                    relay(swgt[:, :], flat(recf[:, :, 2:3]), False)
                else:
                    linear(k)

        @block.tensor
        def _(pe):
            pe.wait_ge(s_const, 6)
            pe.wait_ge(s_cnt, 1)
            nc.tensor.matmul(ps[:, 0, 0:NW], before[:, :], cnt[:, 0, :], start=True, stop=False)
            nc.tensor.matmul(ps[:, 0, 0:NW], ones[:, :], cex[:, 0, :], start=False, stop=True).then_inc(s_tot, 1)
            pe.wait_ge(s_cnt, 2)
            nc.tensor.matmul(ps[0:NW, 1, 0:1], cex[:, 0, :], ones[:, 0:1], start=True, stop=True)
            nc.tensor.matmul(ps[0:NW, 2, 0:1], cex[:, 1, :], ones[:, 0:1], start=True, stop=True).then_inc(s_tot, 1)
            for n, steps in enumerate((CSTEPS, TSTEPS, TSTEPS)):
                pe.wait_ge(s_wind, n + 1)
                nc.tensor.matmul(ps[0:1, 3, 0:NW], wst[:, 1:2], ident[0:NW, 0:NW], start=True, stop=True)
                for j in range(0, steps, 512):
                    m = min(512, steps - j)
                    last = nc.tensor.matmul(ps[0:1, 4 + j // 512, 0:m], ones[0:NW, 0:1], s2v[0:NW, TILES + j:TILES + j + m],
                                            start=True, stop=True)
                last.then_inc(s_wsum, 1)
            pe.wait_ge(s_w, 16 * N_WEIGHTS)
            pe.wait_ge(s_win, 3)
            pe.wait_ge(s_key, 1)

            def up(s, u):
                wait(pe, s_h1, s - 1)
                pe.wait_ge(s_xc[u], 16 * (s // R0 + 1) if isinstance(s, int) else (s - u) * (16 // R0) + 16)
                for h in range(2):
                    last = nc.tensor.matmul(ps[:, 2 * (u % 2) + h, 0:CH // 2], w1s[:, h, :],
                                            xs[:, u, :], start=True, stop=True)
                last.then_inc(s_mm1, 1)

            def mid(s, u):
                wait(pe, s_sl, s - 1)
                pe.wait_ge(s_h1, s + 1)
                nc.tensor.matmul(ps[:, 4 + u, :], onesb[:, :], b2b[:, :], start=True, stop=False)
                for q in range(QT):
                    last = nc.tensor.matmul(ps[:, 4 + u, q * P:(q + 1) * P], h1[:, u, q * P:(q + 1) * P], w2s[:, :],
                                            start=False, stop=q == QT - 1)
                last.then_inc(s_mm2, 1)

            def scat(s, u):
                pe.wait_ge(s_oh0, s + 1)
                pe.wait_ge(s_msg, s + 1)
                wait(pe, s_acc, s - 1)
                for q in range(QT):
                    last = nc.tensor.matmul(ps[:, 6 + u, 0:MW], oh0[:, u, q, :], msg[:, u, q, :],
                                            start=q == 0, stop=q == QT - 1)
                last.then_inc(s_scat, 1)

            up(0, 0)
            up(1, 1)
            mid(0, 0)
            for s in (2, 3):
                up(s, s)
                mid(s - 1, (s - 1) % 2)
                scat(s - 2, s % 2)
            with pe.Fori(1, CSTEPS // R0, 1) as i:
                for u in range(R0):
                    up(i * R0 + u, u)
                    mid(i * R0 + u - 1, (u - 1) % 2)
                    scat(i * R0 + u - 2, u % 2)
            mid(CSTEPS - 1, 1)
            scat(CSTEPS - 2, 0)
            scat(CSTEPS - 1, 1)

            def degree(i, p, first, last):
                pe.wait_ge(s_do, i * 2 + (p + 1))
                for u in range(R):
                    ins = nc.tensor.matmul(ps[:, 7, 0:NW], ohd[:, u, :], ohw[:, u, :], start=first and u == 0,
                                           stop=last and u == R - 1, skip_group_check=True)
                ins.then_inc(s_dm, 1)

            at_n, ev_n = [0], [0]

            def linear(k):
                ws = {0: [0], 1: [1], 2: [2, 3], 3: [4, 5]}[k]
                n_op = LINEARS[k]
                pe.wait_ge(s_op, k + 1)
                srcs = {0: [H], 1: [S1], 2: [S1, H], 3: [S1, H]}[k]

                def turn(g):
                    for o in range(n_op):
                        for j, pair in enumerate(GROUPS[g]):
                            last = nc.tensor.transpose(ps[:, 2 * (g % 2) + o, j * P:(j + 1) * P],
                                                       srcs[o][:, 2 * pair:2 * pair + 2, :].rearrange("p a b -> p (a b)"),
                                                       ident[:, :])
                        last.then_inc(s_tp, 1)

                turn(0)
                for g in range(len(GROUPS)):
                    if g + 1 < len(GROUPS):
                        turn(g + 1)
                    at_n[0] += n_op
                    pe.wait_ge(s_at, at_n[0])
                    if g >= 2:
                        pe.wait_ge(s_ev, ev_n[0] + g - 1)
                    for j in range(len(GROUPS[g])):
                        for o in range(n_op):
                            last = nc.tensor.matmul(ps[:, 4 + g % 2, j * P:(j + 1) * P], at[:, g % 2, o, j * P:(j + 1) * P],
                                                    wns[ws[o]][:, :], start=o == 0, stop=o == n_op - 1)
                    last.then_inc(s_y, 1)
                ev_n[0] += len(GROUPS)

            def add_up(k, i, p):
                pe.wait_ge(s_oh, i * 2 + (k * TURNS + p + 1))
                pe.wait_ge(s_g[p], i * (16 * R) + 16 * R * (k * (TURNS // 2) + 1))
                for u in range(R):
                    ins = nc.tensor.matmul(ps[:, 2 * p + u // 4, D * (u % 4):D * (u % 4 + 1)], oh[:, p, u, :], got[:, p, u, :],
                                           start=True, stop=True)
                ins.then_inc(s_mm, 1)

            for k in range(PASSES):
                if k == 0:
                    linear(0)
                for p in range(2):
                    add_up(k, 0, p)
                    if k == 0:
                        degree(0, p, p == 0, False)
                if k == 0:
                    with pe.Fori(1, DEGREE_TURNS // 2, 1) as i:
                        for p in range(2):
                            add_up(k, i, p)
                            degree(i, p, False, p == 1)
                with pe.Fori(DEGREE_TURNS // 2 if k == 0 else 1, TURNS // 2, 1) as i:
                    for p in range(2):
                        add_up(k, i, p)
                if k:
                    linear(k)

        @block.vector
        def _(dve):
            chain = [0]

            def link(ins):
                chain[0] += 1
                ins.then_inc(s_v, 1)
                dve.wait_ge(s_v, chain[0])

            V = nc.vector
            dve.wait_ge(s_const, 6)
            dve.wait_ge(s_rows, 48)
            link(V.tensor_single_scalar(tmp_i, srow_i, 7, op=ALU.logical_shift_right))
            link(V.tensor_copy(hi_f[:, :], tmp_i))
            link(V.tensor_single_scalar(tmp_i, srow_i, P - 1, op=ALU.bitwise_and))
            link(V.tensor_copy(lo_f[:, :], tmp_i))
            link(V.memset(recf[:, :, 3:4], 0.0))
            V.tensor_copy(rec[:, :, 0:1].rearrange("p t a -> p (t a)"), srow_i)
            V.tensor_copy(rec[:, :, 1:2].rearrange("p t a -> p (t a)"), drow_i)
            link(V.tensor_copy(recf[:, :, 2:3].rearrange("p t a -> p (t a)"), wrow))
            count_n = [0]

            def tally(key):
                n = count_n[0]
                with dve.Fori(0, NW, 1) as w:
                    V.tensor_scalar(mask, key, wcol[:, ds(w, 1)], None, ALU.is_equal, ALU.add,
                                    accum_out=cnt[:, n, ds(w, 1)]).then_inc(s_v, 1)
                    dve.wait_ge(s_v, w + (chain[0] + 1))
                chain[0] += NW
                link(V.memset(cex[:, n, 0:1], 0.0))
                V.tensor_tensor_scan(cex[:, n, 1:NW], ones[:, 0:NW - 1], cnt[:, n, 0:NW - 1], 0.0,
                                     ALU.mult, ALU.add).then_inc(s_cnt, 1)
                count_n[0] += 1
                dve.wait_ge(s_cnt, n + 1)

            tally(hi_f[:, :])
            dve.wait_ge(s_tot, 1)
            link(V.tensor_copy(base[:, :], ps[:, 0, 0:NW]))
            with dve.Fori(0, NW, 1) as w:
                n0 = chain[0]
                V.tensor_scalar(mask, hi_f[:, :], wcol[:, ds(w, 1)], None, ALU.is_equal).then_inc(s_v, 1)
                dve.wait_ge(s_v, w * 3 + (n0 + 1))
                V.tensor_tensor_scan(run, ones[:, 0:1].broadcast_to([P, TILES]), mask, base[:, ds(w, 1)],
                                     ALU.mult, ALU.add).then_inc(s_v, 1)
                dve.wait_ge(s_v, w * 3 + (n0 + 2))
                dve.sem_inc(s_placed, 1)
                V.copy_predicated(pos, mask.bitcast(i32), run).then_inc(s_v, 1)
                dve.wait_ge(s_v, w * 3 + (n0 + 3))
            chain[0] += 3 * NW
            link(V.tensor_scalar(tmp_i, pos, -1.0, None, ALU.add))
            link(V.tensor_single_scalar(slot_i[:, :], tmp_i, P - 1, op=ALU.bitwise_and))
            link(V.tensor_single_scalar(srow_i, tmp_i, 7, op=ALU.logical_shift_right))
            V.scalar_tensor_tensor(out=slot_i[:, :], in0=slot_i[:, :], scalar=float(TILES), in1=srow_i,
                                   op0=ALU.mult, op1=ALU.add).then_inc(s_slot, 1)
            dve.wait_ge(s_slot, 1)
            link(V.tensor_single_scalar(tmp_i, drow_i, 7, op=ALU.logical_shift_right))
            link(V.tensor_copy(pos, tmp_i))
            tally(pos)
            dve.wait_ge(s_tot, 2)
            for n, (bank, shift, last) in enumerate(((2, 9, CHUNKS - 1), (2, 7, TILES - 1), (1, 7, TILES - 1))):
                link(V.tensor_copy(wst_i[:, 0:1], ps[0:NW, bank, 0:1]))
                link(V.tensor_single_scalar(wst_i[:, 1:2], wst_i[:, 0:1], shift, op=ALU.logical_shift_right))
                link(V.tensor_copy(wst[:, 0:1], wst_i[:, 1:2]))
                link(V.tensor_scalar(wst[:, 1:2], wst[:, 0:1], float(last), pidx[0:NW, :], ALU.min, ALU.add))
                steps = CSTEPS if n == 0 else TSTEPS
                V.tensor_scalar(s2v[0:NW, TILES:TILES + steps], iota[0:NW, 0:steps], wst[:, 1:2], None,
                                ALU.is_ge).then_inc(s_wind, 1)
                dve.wait_ge(s_wsum, n + 1)
                V.tensor_copy(wbeg[n][:, :], ps[0:1, 3, 0:NW])
                tab = (dwin_c, dwin_t, swin_t)[n]
                for j in range(0, steps, 512):
                    m = min(512, steps - j)
                    ins = V.tensor_single_scalar(tab[:, j:j + m], ps[0:1, 4 + j // 512, 0:m], -1.0, op=ALU.add)
                ins.then_inc(s_win, 1)
                dve.wait_ge(s_win, n + 1)

            def relay(w, n, q, steps, key):
                s = load(dve, wbeg[n][0:1, ds(w, 1)], steps // q - 1)[0]
                t = less(s, w, TILES // q - 1)
                to, of = s1v[:, ds(s * q, TILES)], s2v[:, ds(t * q, TILES)]
                if key:
                    ins = V.tensor_scalar(to, of, wfirst[:, ds(w, 1)], None, ALU.add)
                else:
                    ins = V.tensor_copy(to, of)
                ins.then_inc(s_lay2, 1)

            link(V.tensor_single_scalar(wfirst[:, :], wcol[:, :], -float(P), op=ALU.mult))
            V.memset(s1v[:, 2 * TILES:WIDE], 0.0)
            link(V.memset(s2v[:, TILES:WIDE], 0.0))
            dve.wait_ge(s_dt, 16)
            link(V.tensor_copy(s2v[:, 0:TILES], dtile_i))
            with dve.Fori(0, NW, 1) as w:
                relay(w, 0, QT, CSTEPS * QT, True)
                dve.wait_ge(s_lay2, w + 1)
            link(V.tensor_copy(dkey_c[:, :], s1v[:, 0:CSTEPS * QT]))
            dve.wait_ge(s_w, 16 * N_WEIGHTS)
            for j in range(3):
                link(V.tensor_scalar(part[:, j:j + 1], pidx[:, :], float(j), None, ALU.is_equal))
            link(V.memset(b2u, 0.0))
            for j in range(3):
                link(V.tensor_copy(b2b[:, :], b2s))
                link(V.tensor_copy(b2t, b2b[:, :]))
                link(V.scalar_tensor_tensor(out=b2u, in0=b2t, scalar=part[:, j:j + 1], in1=b2u, op0=ALU.mult, op1=ALU.add))
                link(V.tensor_tensor(b2s, b2s, b2t, ALU.subtract))
            link(V.tensor_copy(b2b[:, :], b2u))
            V.memset(onesb[:, :], 1.0)
            V.memset(msg[:, :, :, D:MW], 1.0).then_inc(s_key, 1)

            var_n = [0]
            bc = lambda t: t[:, :].rearrange("p (w a) -> p w a", a=1).broadcast_to([P, NWP, D])

            def layernorm():
                link(V.tensor_reduce(mean[:, :], X[:, :, :], axis=AX.X, op=ALU.add))
                link(V.tensor_single_scalar(mean[:, :], mean[:, :], 1.0 / D, op=ALU.mult))
                link(V.tensor_tensor(H[:, :, :], X[:, :, :], bc(mean), ALU.subtract))
                link(V.tensor_tensor(S2[:, :, :], H[:, :, :], H[:, :, :], ALU.mult))
                link(V.tensor_reduce(rstd[:, :], S2[:, :, :], axis=AX.X, op=ALU.add))
                V.tensor_scalar(rstd[:, :], rstd[:, :], 1.0 / D, EPS, ALU.mult, ALU.add).then_inc(s_var, 1)
                var_n[0] += 1
                dve.wait_ge(s_std, var_n[0])
                link(V.reciprocal(rstd[:, :], rstd[:, :]))
                link(V.scalar_tensor_tensor(out=H[:, :, :], in0=H[:, :, :], scalar=0.0, in1=bc(rstd),
                                            op0=ALU.max, op1=ALU.mult))

            dve.wait_ge(s_x, 16)
            layernorm()
            link(V.memset(ACC[:, :, :], 0.0))

            iota_q = iota[:, 0:P].rearrange("p (a n) -> p a n", a=1)

            def onehots(s, u):
                wait(dve, s_scat, s - 1)
                V.tensor_tensor(oh0[:, u, :, :], iota_q.broadcast_to([P, QT, P]),
                                dkey_c[:, ds(s * QT, QT)].rearrange("p (q a) -> p q a", a=1).broadcast_to([P, QT, P]),
                                ALU.is_equal).then_inc(s_oh0, 1)

            def message(s, u):
                dve.wait_ge(s_sl, s + 1)
                wait(dve, s_scat, s - 1)
                V.scalar_tensor_tensor(out=msg[:, u, :, 0:D], in0=th[:, u, :, :], scalar=1.0, in1=sl[:, u, :, :],
                                       op0=ALU.add, op1=ALU.mult).then_inc(s_msg, 1)

            def add_chunk(s, u, w):
                dve.wait_ge(s_scat, s + 1)
                wait(dve, s_acc, s)
                to = accv[:, ds(w * MW, MW)]
                V.tensor_tensor(to, to, ps[:, 6 + u, 0:MW], ALU.add).then_inc(s_acc, 1)

            onehots(0, 0)
            onehots(1, 1)
            message(0, 0)
            w = windows(dve, dwin_c, 0, R0)
            for s in (2, 3):
                add_chunk(s - 2, s % 2, w[s - 2])
                onehots(s, s % 2)
                message(s - 1, (s - 1) % 2)

            def four(i):
                w = windows(dve, dwin_c, i * R0 - 2, R0)
                for u in range(R0):
                    add_chunk(i * R0 + u - 2, u % 2, w[u])
                    onehots(i * R0 + u, u % 2)
                    message(i * R0 + u - 1, (u - 1) % 2)

            link(V.tensor_copy(s2v[:, 0:TILES], dtile_i))
            with dve.Fori(1, NW + 1, 1) as i:
                four(i)
                dve.wait_ge(s_lay2, i + (NW - 1))
                relay(i - 1, 1, 1, TSTEPS, True)
            dve.wait_ge(s_lay2, 2 * NW)
            link(V.tensor_copy(dkey[:, :], s1v[:, 0:TSTEPS]))
            dve.wait_ge(s_st, 16)
            link(V.tensor_copy(s2v[:, 0:TILES], stile_i))
            with dve.Fori(NW + 1, 2 * NW + 1, 1) as i:
                four(i)
                dve.wait_ge(s_lay2, i + (NW - 1))
                relay(i - (NW + 1), 1, 1, TSTEPS, False)
            dve.wait_ge(s_lay2, 3 * NW)
            link(V.tensor_copy(dget[:, :], s1v[:, 0:TSTEPS]))
            with dve.Fori(2 * NW + 1, CSTEPS // R0, 1) as i:
                four(i)
            w = windows(dve, dwin_c, CSTEPS - 2, 2)
            add_chunk(CSTEPS - 2, 0, w[0])
            message(CSTEPS - 1, 1)
            add_chunk(CSTEPS - 1, 1, w[1])

            def degree(i, p):
                t = i * 2 + p
                wait(dve, s_dm, t)
                wide = lambda v, n: v.rearrange("p (r a) -> p r a", a=1).broadcast_to([P, R, n])
                V.tensor_tensor(ohd, iota_q.broadcast_to([P, R, P]), wide(lo_f[:, ds(t * R, R)], P), ALU.is_equal)
                V.tensor_tensor(ohw[:, :, :], wcol[:, :].rearrange("p (a n) -> p a n", a=1).broadcast_to([P, R, NW]),
                                wide(hi_f[:, ds(t * R, R)], NW), ALU.is_equal).then_inc(s_dp, 1)
                dve.wait_ge(s_dp, t + 1)
                V.tensor_tensor(ohw[:, :, :], ohw[:, :, :], wide(wgt[:, ds(t * R, R)], NW), ALU.mult).then_inc(s_do, 1)

            dve.wait_ge(s_acc, CSTEPS)
            dve.wait_ge(s_scat, CSTEPS)
            V.tensor_copy(wgt, recf[:, :, 2:3].rearrange("p t a -> p (t a)")).then_inc(s_kept, 1)
            dve.wait_ge(s_kept, 1)
            link(V.tensor_copy(count[:, :], ACC[:, :, D]))
            link(V.tensor_tensor(X[:, :, :], X[:, :, :], H[:, :, :], ALU.add))
            link(V.scalar_tensor_tensor(out=X[:, :, :], in0=ACC[:, :, 0:D], scalar=0.5, in1=X[:, :, :],
                                        op0=ALU.mult, op1=ALU.add))
            layernorm()

            y_n = [0]

            def products(evac):
                for g, pairs in enumerate(GROUPS):
                    y_n[0] += 1
                    dve.wait_ge(s_y, y_n[0])
                    w0, nw = 2 * pairs[0], 2 * len(pairs)
                    yv = ps[:, 4 + g % 2, 0:nw * D].rearrange("p (w d) -> p w d", d=D)
                    evac(slice(w0, w0 + nw), nw, yv).then_inc(s_ev, 1)
                dve.wait_ge(s_ev, y_n[0])

            def degrees(sc, deg):
                link(V.tensor_scalar(mean[:, :], deg, 0.0, None, ALU.is_gt))
                link(V.tensor_tensor(sc[:, :], deg, mean[:, :], ALU.mult))
                link(V.scalar_tensor_tensor(out=sc[:, :], in0=mean[:, :], scalar=-1.0, in1=sc[:, :],
                                            op0=ALU.mult, op1=ALU.add))
                V.tensor_scalar(sc[:, :], sc[:, :], 1.0, None, ALU.add).then_inc(s_var, 1)
                var_n[0] += 1
                dve.wait_ge(s_std, var_n[0])
                link(V.reciprocal(sc[:, :], sc[:, :]))
                link(V.tensor_tensor(sc[:, :], sc[:, :], mean[:, :], ALU.mult))

            bias = lambda b, nw: b[:, :].rearrange("p (a d) -> p a d", a=1).broadcast_to([P, nw, D])

            def spread(k):
                tab = swin_t if k == 1 else dwin_t
                key = skey if k == 1 else dkey

                def onehot(i, p):
                    t = i * 2 + p
                    wait(dve, s_mm, k * TURNS + i * 2 + p - 1)
                    wide = lambda v: v.rearrange("p (r a) -> p r a", a=1).broadcast_to([P, R, P])
                    ins = V.tensor_tensor(oh[:, p, :, :], iota_q.broadcast_to([P, R, P]), wide(key[:, ds(t * R, R)]),
                                          ALU.is_equal)
                    if k == 1:
                        ins.then_inc(s_wt, 1)
                        dve.wait_ge(s_wt, t + 1)
                        ins = V.tensor_tensor(oh[:, p, :, :], oh[:, p, :, :], wide(swgt[:, ds(t * R, R)]), ALU.mult)
                    ins.then_inc(s_oh, 1)

                def add(i, p):
                    t = i * 2 + p
                    turn = i * 2 + (k * TURNS + p + 1)
                    if not isinstance(i, int):
                        turn = dve.snap(turn)
                    w = windows(dve, tab, t * R, R)
                    dve.wait_ge(s_mm, turn)
                    for u in range(R):
                        wait(dve, s_add[u - 1], turn if u else turn - 1)
                        to = ACC[:, ds(w[u], 1), 0:D].rearrange("p a b -> p (a b)")
                        V.tensor_tensor(to, to, ps[:, 2 * p + u // 4, D * (u % 4):D * (u % 4 + 1)], ALU.add).then_inc(s_add[u], 1)

                onehot(0, 0)
                onehot(0, 1)
                if k == 0:
                    degree(0, 0)
                add(0, 0)
                if k == 0:
                    degree(0, 1)
                    with dve.Fori(1, DEGREE_TURNS // 2, 1) as i:
                        onehot(i, 0)
                        add(i - 1, 1)
                        degree(i, 0)
                        onehot(i, 1)
                        add(i, 0)
                        degree(i, 1)
                with dve.Fori(DEGREE_TURNS // 2 if k == 0 else 1, TURNS // 2, 1) as i:
                    onehot(i, 0)
                    add(i - 1, 1)
                    onehot(i, 1)
                    add(i, 0)
                add(TURNS // 2 - 1, 1)
                dve.wait_ge(s_add[R - 1], (k + 1) * TURNS)

            link(V.tensor_scalar(scale3[:, :], count[:, :], 1.0, None, ALU.add))
            degrees(scale1, scale3[:, :])
            V.memset(scale3[:, 0:1], 0.0).then_inc(s_op, 1)
            sc1 = lambda ww, nw: scale1[:, ww].rearrange("p (w a) -> p w a", a=1).broadcast_to([P, nw, D])
            products(lambda ww, nw, y: V.tensor_tensor(S1[:, ww, :], y, sc1(ww, nw), ALU.mult))
            V.tensor_copy(ACC[:, :, 0:D], S1[:, :, :]).then_inc(s_tab, 1)
            spread(0)
            dve.wait_ge(s_lay, 3 * (NW + 2))
            link(V.tensor_tensor(S1[:, :, :], ACC[:, :, 0:D], bc(scale1), ALU.mult))
            link(V.tensor_tensor(S1[:, :, :], S1[:, :, :], bias(bns[0], NWP), ALU.add))
            link(V.scalar_tensor_tensor(out=X[:, :, :], in0=S1[:, :, :], scalar=0.0, in1=X[:, :, :],
                                        op0=ALU.max, op1=ALU.add))
            layernorm()
            dve.wait_ge(s_dm, DEGREE_TURNS)
            link(V.memset(scale3[:, :], 1.0))
            link(V.tensor_scalar(scale3[:, 0:NW], ps[:, 7, 0:NW], 1.0, None, ALU.add))
            degrees(scale2, scale3[:, :])
            link(V.tensor_tensor(S1[:, :, :], H[:, :, :], bc(scale2), ALU.mult))
            V.tensor_copy(ACC[:, :, 0:D], S1[:, :, :]).then_inc(s_tab, 1)
            spread(1)
            V.tensor_tensor(S1[:, :, :], ACC[:, :, 0:D], bc(scale2), ALU.mult).then_inc(s_op, 1)
            dve.wait_ge(s_op, 2)
            link(V.tensor_tensor(X[:, :, :], X[:, :, :], bias(bns[1], NWP), ALU.add))
            products(lambda ww, nw, y: V.tensor_tensor(X[:, ww, :], X[:, ww, :], y, ALU.add))
            layernorm()
            link(V.tensor_scalar(scale3[:, :], count[:, :], 1.0, None, ALU.max))
            link(V.reciprocal(scale3[:, :], scale3[:, :]))
            V.memset(ACC[:, :, :], 0.0).then_inc(s_tab, 1)
            dve.wait_ge(s_tab, 3)
            spread(2)
            V.tensor_tensor(S1[:, :, :], ACC[:, :, 0:D], bc(scale3), ALU.mult).then_inc(s_op, 1)
            products(lambda ww, nw, y: V.tensor_tensor(S2[:, ww, :], y, bias(bns[2], nw), ALU.add))
            link(V.tensor_scalar(H[:, :, :], S2[:, :, :], 0.0, None, ALU.max))
            V.memset(ACC[:, :, :], 0.0).then_inc(s_tab, 1)
            dve.wait_ge(s_tab, 4)
            spread(3)
            V.tensor_tensor(S1[:, :, :], ACC[:, :, 0:D], bc(scale3), ALU.mult).then_inc(s_op, 1)
            link(V.tensor_tensor(X[:, :, :], X[:, :, :], bias(bns[3], NWP), ALU.add))
            products(lambda ww, nw, y: V.tensor_tensor(X[:, ww, :], X[:, ww, :], y, ALU.add))
            V.memset(mean[:, 0:1], 0.0).then_inc(s_fin, 1)


def kernel(**inputs):
    import numpy as np
    import concourse.bacc as bacc
    from concourse.bass_utils import run_bass_kernel_spmd as run

    def a(name):
        return np.ascontiguousarray(inputs[name])

    def padded(v, fill):
        return np.concatenate([v, np.full((EDGES - N_EDGES,), fill, v.dtype)])

    def twice(w):
        both = np.zeros((P, P), w.dtype)
        both[0:D, 0:D] = w
        both[D:P, D:P] = w
        return both

    def rows(b):
        return np.ascontiguousarray(np.broadcast_to(b, (P, D)))

    x = np.zeros((NWP * P, D), np.float32)
    x[0:N_NODES] = a("x")
    e = np.zeros((EDGES, D), np.float32)
    e[0:N_EDGES] = a("edge_attr_64")
    src, dst = padded(a("src"), DUMMY), padded(a("dst"), DUMMY)
    w = padded(a("edge_weight"), 0)
    w2g2 = np.zeros((P, P), np.float32)
    w2g2[0:D, 0:D] = a("L0_gnn_W2")
    w2g2[D:P, D:P] = a("L0_gnn_G2")
    zero = np.zeros((D, P), np.float32)
    w1g1 = np.concatenate([a("L0_gnn_W1"), a("L0_gnn_G1")], axis=1)
    arrays = {
        "x": x.reshape(NWP, P, D).transpose(1, 0, 2),
        "edge_t": e.reshape(CHUNKS, 2, CH // 2, D).transpose(0, 1, 3, 2).reshape(CHUNKS, P, CH // 2),
        "dst_tiles": dst.reshape(TILES, P).T, "src_tiles": src.reshape(TILES, P).T,
        "src_rows": src.reshape(P, TILES), "dst_rows": dst.reshape(P, TILES), "w_rows": w.reshape(P, TILES),
        "w1g1": np.stack([np.concatenate([w1g1, zero]), np.concatenate([zero, w1g1])], axis=1).reshape(P, 2 * P),
        "w2g2": w2g2,
        "b1g1": np.concatenate([a("L0_gnn_b1"), a("L0_gnn_g1")]).reshape(P, 1),
        "b2g2": np.tile(np.concatenate([a("L0_gnn_b2"), a("L0_gnn_g2")]), (P, QT)),
        "w_gcn": twice(a("L1_gnn_W")), "w_l2": twice(a("L2_gnn_W").T),
        "w_l0": twice(a("L3_gnn_Wl0")), "w_r0": twice(a("L3_gnn_Wr0")),
        "w_l1": twice(a("L3_gnn_Wl1")), "w_r1": twice(a("L3_gnn_Wr1")),
        "b_gcn": rows(a("L1_gnn_b")), "b_l2": rows(a("L2_gnn_b")),
        "b_l0": rows(a("L3_gnn_bl0")), "b_l1": rows(a("L3_gnn_bl1")),
    }
    nc = bacc.Bacc("TRN2", target_bir_lowering=False, num_devices=1)
    sent, args = {}, []
    for name, v in arrays.items():
        sent[f"in_{name}"] = np.ascontiguousarray(v)
        args.append(nc.dram_tensor(f"in_{name}", v.shape, mybir.dt.from_np(v.dtype), kind="ExternalInput").ap())
    args.append(nc.dram_tensor("out_0", (N_NODES, D), mybir.dt.float32, kind="ExternalOutput").ap())
    gnn_kernel(nc, *args)
    return run(nc, [sent], core_ids=[0]).results[0]["out_0"]
```

```python
import concourse.bass as bass
from concourse import mybir
from contextlib import ExitStack

P = 128
N_NODES, N_EDGES, D = 6250, 200000, 64
NW = -(-N_NODES // P)
NWP = NW + NW % 2
NODES = NW * P
DUMMY = NODES - 1
CH = 512
R = 8
EDGES = -(-N_EDGES // (R * P)) * R * P
TILES = EDGES // P
CHUNKS = EDGES // CH
QT = CH // P
CSTEPS = CHUNKS + NW - 1
TSTEPS = TILES + NW - 1
R0 = 4
TURNS = TSTEPS // R
BLOCKS = NW * NW
BSTEPS = TILES + BLOCKS - 1
G = 4
UNITS = BSTEPS // G
UNITS0 = TILES // R // 2 * 4
ROWS = BSTEPS // P
SPAN = 512
DG = NW // 4
PIECES = [6] * 7 + [7]
TCH = -(-TILES // P)
SPARE = (DG + 1) * NW * P * 4
OVER = 65536 // NW + 1
DEGREE_TURNS = TILES // R
WIDE = 3328
MW = D + 1
EPS = 1e-5


def ds(start, size):
    return bass.DynSlice(start, size)


def wait(eng, sem, value):
    if not isinstance(value, int) or value > 0:
        eng.wait_ge(sem, value)


def gnn_kernel(nc, x, edge_t, dst_tiles, src_tiles, src_rows, dst_rows, w_rows, w1g1, w2g2, b1g1, b2g2,
               w_gcn, w_l2, w_l0, w_r0, w_l1, w_r1, b_gcn, b_l2, b_l0, b_l1, out):
    f32, bf16, i32 = mybir.dt.float32, mybir.dt.bfloat16, mybir.dt.int32
    ALU, ACT, AX = mybir.AluOpType, mybir.ActivationFunctionType, mybir.AxisListType
    ctx = ExitStack()
    with ctx:
        def sb(name, shape, dt=f32):
            return ctx.enter_context(nc.sbuf_tensor(name, shape, dt))

        def sem(name):
            return ctx.enter_context(nc.semaphore(name))

        records = nc.dram_tensor("records", (EDGES, 4), i32).ap()
        table = nc.dram_tensor("table", (NODES, D), f32).ap()
        dense = nc.dram_tensor("dense", (SPARE + (2 * G + 1) * P * 4, P), f32).ap()
        places = nc.dram_tensor("places", (1, BSTEPS), i32).ap()

        X = sb("X", [P, NWP, D])
        H = sb("H", [P, NWP, D])
        ACC = sb("ACC", [P, NWP, MW])
        s12 = sb("s12", [P, 2 * WIDE])
        s1v, s2v = s12[:, 0:WIDE], s12[:, WIDE:2 * WIDE]
        S1 = s1v[:, 0:NWP * D].rearrange("p (a b) -> p a b", b=D)
        S2 = s2v[:, 0:NWP * D].rearrange("p (a b) -> p a b", b=D)
        count = sb("count", [P, NWP])
        scale1 = sb("scale1", [P, NWP])
        scale2 = sb("scale2", [P, NWP])
        scale3 = sb("scale3", [P, NWP])
        mean = sb("mean", [P, NWP])
        rstd = sb("rstd", [P, NWP])
        iota = sb("iota", [P, TSTEPS])
        dkey_c = sb("dkey_c", [P, CSTEPS * QT])
        dkey = sb("dkey", [P, TSTEPS])
        dget = sb("dget", [P, TSTEPS], i32)
        rec = sb("rec", [P, TILES, 4], i32)
        recf = rec[:, :, :].bitcast(f32)
        laid = sb("laid", [P, 3 * TSTEPS])
        skey = laid[:, 0:TSTEPS]
        sget = laid[:, TSTEPS:2 * TSTEPS].bitcast(i32)
        swgt = laid[:, 2 * TSTEPS:3 * TSTEPS]
        hilo = sb("hilo", [P, 2 * TILES])
        hi_f, lo_f = hilo[:, 0:TILES], hilo[:, TILES:2 * TILES]
        slot_i = sb("slot_i", [P, TILES], i32)
        accv = ACC[:, :, :].rearrange("p a b -> p (a b)")
        srow_i = s1v[:, 0:TILES].bitcast(i32)
        drow_i = s1v[:, TILES:2 * TILES].bitcast(i32)
        wrow = s2v[:, 0:TILES]
        mask = s2v[:, TILES:2 * TILES]
        run = skey[:, 0:TILES]
        pos = accv[:, 0:TILES]
        tmp_i = accv[:, TILES:2 * TILES].bitcast(i32)
        dtile_i = swgt[:, 0:TILES].bitcast(i32)
        stile_i = sget[:, 0:TILES]
        ident = sb("ident", [P, P])
        before = sb("before", [P, P])
        ones = sb("ones", [P, P])
        wcol = sb("wcol", [P, NW])
        wfirst = sb("wfirst", [P, NW])
        pidx = sb("pidx", [P, 1])
        cnt = sb("cnt", [P, 2, NW])
        cex = sb("cex", [P, 2, NW])
        base = sb("base", [P, NW])
        mark = sb("mark", [32, P])
        block_at = sb("block_at", [32, P])
        parts = sb("parts", [P, ROWS // 4 * 4 + TCH])
        wst_i = sb("wst_i", [NW, 4], i32)
        wst = sb("wst", [NW, 4])
        wbeg = [sb(f"wbeg{i}", [1, NW], i32) for i in range(2)]
        dwin_c = sb("dwin_c", [1, CSTEPS], i32)
        place_s = dwin_c[:, 0:6 * G]
        place_p = dwin_c[:, 6 * G:12 * G]
        dwin_t = sb("dwin_t", [1, TSTEPS], i32)
        swin_t = sb("swin_t", [1, TSTEPS], i32)
        w1s = sb("w1s", [P, 2, P])
        w2s = sb("w2s", [P, P])
        b1s = sb("b1s", [P, 1])
        b2s = H[:, 0:CH // D, :].rearrange("p a b -> p (a b)")
        b2t = H[:, CH // D:2 * CH // D, :].rearrange("p a b -> p (a b)")
        b2u = H[:, 2 * CH // D:3 * CH // D, :].rearrange("p a b -> p (a b)")
        b2b = sb("b2b", [P, CH], bf16)
        onesb = sb("onesb", [P, P], bf16)
        part = sb("part", [P, 3])
        wns = [sb(f"wn{i}", [P, P]) for i in range(6)]
        bns = [sb(f"bn{i}", [P, D]) for i in range(4)]
        ring = sb("ring", [P, (UNITS - UNITS0) * G])
        xs = ring[:, 0:2 * CH].rearrange("p (r e) -> p r e", r=R0)
        h1 = ring[:, 2 * CH:4 * CH].rearrange("p (r e) -> p r e", r=2)
        at = ring[:, 0:4 * CH].rearrange("p (a b e) -> p a b e", a=2, b=2)
        mlp = sb("mlp", [P, 2 * QT * (2 * D + MW)])
        quarters = lambda at, n: mlp[:, at * 2 * QT:(at + n) * 2 * QT].rearrange("p (a q d) -> p a q d", a=2, q=QT)
        sl, th, msg = quarters(0, D), quarters(D, D), quarters(2 * D, MW)
        ohd = mlp[:, 0:R * P].rearrange("p (r n) -> p r n", r=R)
        bone_iota = mlp[:, R * P:R * P + G * P].bitcast(bf16).rearrange("p (n j) -> p n j", j=2 * G)
        wgt = dkey_c[:, 0:TILES]
        idx_s = sb("idx_s", [P, 2, R], i32)
        rec_s = sb("rec_s", [P, 2, R, 4], i32)
        got = sb("got", [P, 2, R, D])
        oh = sb("oh", [P, 2, R, P])
        oh0 = oh[:, 0, :, :].rearrange("p (a q) n -> p a q n", q=QT)
        hone = oh[:, 1, :, :].rearrange("p a b -> p (a b)")[:, 0:2 * R * NW].bitcast(bf16).rearrange(
            "p (r k u n) -> p r k u n", r=2, k=2, u=R)
        bhi = s12[0:NW, 2 * WIDE - NW * 16:2 * WIDE].bitcast(bf16).rearrange("p (w n) -> p w n", w=NW)
        blo = s12[0:NW, 2 * WIDE - NW * 80:2 * WIDE - NW * 16].bitcast(bf16).rearrange("p (w n) -> p w n", w=NW)
        ohw = sb("ohw", [P, R, NW])
        flat = recf.rearrange("p t k -> p (t k)")
        same = flat[:, 0:BSTEPS + 1]
        sums = flat[:, BSTEPS + 1:BSTEPS + 1 + 2 * G * P].rearrange("p (r j n) -> p r j n", r=2, j=G)
        bone = flat[:, BSTEPS + 1 + 2 * G * P:BSTEPS + 1 + 4 * G * P].bitcast(bf16).rearrange(
            "p (r n j) -> p r n j", r=2, j=2 * G)
        bkey = [slot_i[:, :].bitcast(bf16).rearrange("p (u j) -> p u j", j=2 * G),
                ring[:, :].bitcast(bf16).rearrange("p (u j) -> p u j", j=2 * G)]
        tt = s12[:, 0:3 * TCH * P].rearrange("p (k c e) -> p k c e", k=3, c=TCH)
        two = [tt[:, k, :, :].rearrange("p c e -> p (c e)").bitcast(bf16).rearrange("p (h n) -> p h n", h=2) for k in range(3)]
        sel_at, third_at = 3 * TCH * P, 3 * TCH * P + 3 * SPAN // 2
        sel = s12[:, sel_at:third_at].bitcast(bf16).rearrange("p (r n) -> p r n", r=3)
        third = s12[:, third_at:third_at + TCH * P // 2].bitcast(bf16)
        tile_parts = [[two[0][:, 0, :], two[0][:, 1, :]], [two[1][:, 0, :], two[1][:, 1, :]],
                      [two[2][:, 0, :], two[2][:, 1, :], third]]
        tmp = [H[:, SPAN // D * i:SPAN // D * (i + 1), :].rearrange("p a b -> p (a b)") for i in range(6)]
        pieces = [flat[:, 0:6 * SPAN], flat[:, 6 * SPAN:12 * SPAN], hilo[:, 0:6 * SPAN], laid[:, 0:7 * SPAN]]
        agg_t = ring[0:D, 2 * SPAN:3 * SPAN]
        ps = ctx.enter_context(nc.psum_tensor("ps", [P, 8, 512], f32))

        s_w, s_x, s_dt, s_st, s_rows = sem("s_w"), sem("s_x"), sem("s_dt"), sem("s_st"), sem("s_rows")
        s_const, s_pc = sem("s_const"), sem("s_pc")
        s_v = sem("s_v")
        s_cnt, s_tot, s_wind, s_wsum, s_win = (sem(n) for n in ("s_cnt", "s_tot", "s_wind", "s_wsum", "s_win"))
        s_slot, s_stg, s_sc = sem("s_slot"), sem("s_stg"), [sem(f"s_sc{i}") for i in range(2)]
        s_xc = [sem(f"s_xc{i}") for i in range(R0)]
        s_mm1, s_h1, s_mm2, s_sl, s_msg, s_oh0, s_scat, s_acc = (sem(n) for n in (
            "s_mm1", "s_h1", "s_mm2", "s_sl", "s_msg", "s_oh0", "s_scat", "s_acc"))
        s_dp, s_do, s_dm = sem("s_dp"), sem("s_do"), sem("s_dm")
        s_rec = sem("s_rec")
        s_idx, s_g = ([sem(f"{n}{i}") for i in range(2)] for n in ("s_idx", "s_g"))
        s_oh, s_mm, s_add = sem("s_oh"), sem("s_mm"), [sem(f"s_add{i}") for i in range(R)]
        s_key, s_lay, s_kept = sem("s_key"), sem("s_lay"), sem("s_kept")
        s_hp, s_hm, s_bh, s_bhm, s_pre, s_prem = (sem(n) for n in ("s_hp", "s_hm", "s_bh", "s_bhm", "s_pre", "s_prem"))
        s_cast, s_tr, s_te, s_ex, s_exm, s_sel, s_selm = (sem(n) for n in (
            "s_cast", "s_tr", "s_te", "s_ex", "s_exm", "s_sel", "s_selm"))
        s_pl, s_pld, s_pls, s_ppls, s_wt = sem("s_pl"), [sem(f"s_pld{i}") for i in range(2)], sem("s_pls"), sem("s_ppls"), sem("s_wt")
        s_bo, s_bm, s_bs, s_bw = sem("s_bo"), sem("s_bm"), sem("s_bs"), [sem(f"s_bw{i}") for i in range(2)]
        s_piece, s_pd, s_gs, s_gt, s_gb = [sem(f"s_piece{i}") for i in range(4)], sem("s_pd"), sem("s_gs"), sem("s_gt"), sem("s_gb")
        s_fetched, s_turned = sem("s_fetched"), sem("s_turned")
        s_begun, s_placed = sem("s_begun"), sem("s_placed")
        s_var, s_std = sem("s_var"), sem("s_std")
        s_op, s_tp, s_at, s_y, s_ev = sem("s_op"), sem("s_tp"), sem("s_at"), sem("s_y"), sem("s_ev")
        s_tab, s_tst, s_fin, s_out = sem("s_tab"), sem("s_tst"), sem("s_fin"), sem("s_out")
        block = ctx.enter_context(nc.Block())

        FETCHES = DEGREE_TURNS // 2 + TURNS // 2
        N_WEIGHTS = 4 + 6 + 4
        PASSES = 4
        GROUPS = [list(range(g, min(g + 4, NWP // 2))) for g in range(0, NWP // 2, 4)]
        LINEARS = [1, 1, 2, 2]

        def load(eng, ap, top):
            _, values = nc.values_load_multi_w_load_instructions(
                ap, engines=[eng.engine], min_val=0, max_val=top,
                skip_runtime_bounds_check_because="counts of windows that have begun, the first of which always has, and steps at which they begin")
            return values

        def windows(eng, tab, s, n):
            return load(eng, tab[0:1, ds(s, n)], NW - 1)

        def less(a, b, top):
            return nc.s_assert_within(a - b, 0, top, skip_runtime_bounds_check_because="each step goes to a window or to a tile, and window w begins w steps or more after the first")

        def fetch(eng, to, s, n, count):
            eng.dma_start(to[0:1, 0:count * G], places[0:1, ds(n * G, count * G)]).then_inc(s, 16)

        def fetched(eng, s, m):
            eng.wait_ge(s, m * 16 + 16)
            eng.sem_inc(s_fetched, 1)

        def write(eng, table_s, n, v, parity, half):
            slot = (v + parity) % 2
            at_rows = load(eng, table_s[0:1, v * G + 2 * half:v * G + 2 * half + 2], SPARE + 2 * G * P * 4 - 1)
            eng.wait_ge(s_bs, n * G + (2 * half + 2))
            for j in range(2):
                eng.dma_start(dense[ds(at_rows[j], P * 4), :].rearrange("(p s) n -> p (s n)", p=P)[:, 0:P],
                              sums[:, slot, 2 * half + j, :]).then_inc(s_bw[slot], 16)

        @block.sync
        def _(sp):
            sp.dma_start(srow_i, src_rows).then_inc(s_rows, 16)
            sp.dma_start(drow_i, dst_rows).then_inc(s_rows, 16)
            sp.dma_start(wrow, w_rows).then_inc(s_rows, 16)
            sp.dma_start(X[:, :, :], x).then_inc(s_x, 16)
            sp.dma_start(dtile_i, dst_tiles).then_inc(s_dt, 16)
            sp.dma_start(stile_i, src_tiles).then_inc(s_st, 16)
            sp.dma_start(w1s[:, :, :], w1g1.rearrange("p (h n) -> p h n", h=2)).then_inc(s_w, 16)
            sp.dma_start(b2s, b2g2).then_inc(s_w, 16)
            for to, of in [(w2s, w2g2), (b1s, b1g1)] + list(
                    zip(wns, (w_gcn, w_l2, w_l0, w_r0, w_l1, w_r1))) + list(zip(bns, (b_gcn, b_l2, b_l0, b_l1))):
                sp.dma_start(to[:, :], of).then_inc(s_w, 16)
            sp.wait_ge(s_win, 1)

            def chunk(s, u, w):
                c = less(s, w, CHUNKS - 1)
                wait(sp, s_mm1, s - R0 + 1)
                sp.dma_start(xs[:, u, :], edge_t[ds(c, 1), :, :].rearrange("a p e -> (a p) e")).then_inc(s_xc[u], 16)

            for s, w in enumerate(windows(sp, dwin_c, 0, R0)):
                chunk(s, s, w)
            with sp.Fori(1, CSTEPS // R0, 1) as i:
                for u, w in enumerate(windows(sp, dwin_c, i * R0, R0)):
                    chunk(i * R0 + u, u, w)
            for p in range(2):
                sp.wait_ge(s_sc[p], 16 * R * (TILES // R // 2))
            sp.wait_ge(s_kept, 1)
            sp.dma_start(rec[:, :, :], records.rearrange("(p t) k -> p t k", p=P)).then_inc(s_rec, 16)
            for k in range(2):
                sp.wait_ge(s_tab, k + 1)
                sp.dma_start(table.rearrange("(w p) f -> p w f", p=P), S1[:, 0:NW, :]).then_inc(s_tst, 16)
                rows = sget if k == 1 else dget

                def stage(i, p):
                    wait(sp, s_mm, k * TURNS + i * 2 + p - 1)
                    sp.dma_start(idx_s[:, p, :], rows[:, ds((i * 2 + p) * R, R)]).then_inc(s_idx[p], 16)

                def turn(i, units, number, last=False):
                    if units:
                        first, count = units
                        fetch(sp, place_p, s_ppls, first, count)
                    stage(i, 1)
                    if units:
                        fetched(sp, s_ppls, number)
                        for v in range(count // 2):
                            write(sp, place_p, first + v, v, 0, 1)
                    if not last:
                        stage(i + 1, 0)
                    if units:
                        for v in range(count // 2, count):
                            write(sp, place_p, first + v, v, 0, 1)

                stage(0, 0)
                stage(0, 1)
                stage(1, 0)
                last = DEGREE_TURNS // 2
                if k == 0:
                    for p in range(2):
                        sp.wait_ge(s_pld[p], 16 * ((-(-BSTEPS // SPAN) + 1 - p) // 2))
                    with sp.Fori(1, last, 1) as i:
                        turn(i, (i * 4 - 4, 4), i - 1)
                    stage(last, 1)
                    fetch(sp, place_p, s_ppls, UNITS0 - 4, 2)
                    sp.wait_ge(s_ppls, 16 * last)
                    for v in range(2):
                        write(sp, place_p, UNITS0 - 4 + v, v, 0, 1)
                    stage(last + 1, 0)
                    for i in range(last + 1, TURNS // 2):
                        turn(i, None, 0, i == TURNS // 2 - 1)
                else:
                    with sp.Fori(1, TURNS // 2 - 1, 1) as i:
                        turn(i, (i * 6 + (UNITS0 - 8), 6), i + (last - 1))
                    turn(TURNS // 2 - 1, (UNITS - 8, 6), TURNS // 2 - 2 + last, True)
                    fetch(sp, place_p, s_ppls, UNITS - 2, 2)
                    sp.wait_ge(s_ppls, 16 * FETCHES)
                    for v in range(2):
                        write(sp, place_p, UNITS - 2 + v, v, 0, 1)
            for r in range(2):
                sp.wait_ge(s_bw[r], 16 * G * (UNITS // 2))
            sp.wait_ge(s_tab, 3)

            def group(kk, g, n):
                for q, size in enumerate(PIECES):
                    m = n * 8 + q
                    wait(sp, s_pd, m - 3)
                    rows = dense[ds(g * (NW * P * 4) + 6 * q * P * 4, size * P * 4), :].rearrange("(s p w) n -> p s (w n)", p=P, w=4)
                    cols = SPAN if isinstance(g, int) is False or g < DG else P
                    sp.dma_start(pieces[q % 4][:, 0:size * cols].rearrange("p (s n) -> p s n", s=size),
                                 rows[:, :, 0:cols]).then_inc(s_piece[q % 4], 16)

            for kk in range(2):
                first = kk * (DG + 1)
                group(kk, 0, first)
                with sp.Fori(1, DG, 1) as g:
                    group(kk, g, g + first)
                group(kk, DG, DG + first)
            sp.wait_ge(s_fin, 1)
            full = N_NODES // P
            sp.dma_start(out[0:full * P, :].rearrange("(w p) f -> p w f", p=P), X[:, 0:full, :]).then_inc(s_out, 16)
            sp.dma_start(out[full * P:N_NODES, :], X[0:N_NODES - full * P, full, :]).then_inc(s_out, 16)
            sp.wait_ge(s_out, 32)

        @block.gpsimd
        def _(pool):
            nc.gpsimd.iota(iota[:, :], [[1, TSTEPS]], base=0, channel_multiplier=0,
                           allow_small_or_imprecise_dtypes=True).then_inc(s_const, 1)
            nc.gpsimd.iota(wcol[:, :], [[1, NW]], base=0, channel_multiplier=0,
                           allow_small_or_imprecise_dtypes=True).then_inc(s_const, 1)
            nc.gpsimd.iota(pidx[:, :], [[0, 1]], base=0, channel_multiplier=1,
                           allow_small_or_imprecise_dtypes=True).then_inc(s_const, 1)
            nc.gpsimd.memset(ones[:, :], 1.0).then_inc(s_const, 1)
            nc.gpsimd.memset(ident[:, :], 0.0).then_inc(s_pc, 1)
            nc.gpsimd.memset(before[:, :], 1.0).then_inc(s_pc, 1)
            pool.wait_ge(s_pc, 2)
            nc.gpsimd.affine_select(out=ident[:, :], in_=ident[:, :], compare_op=ALU.not_equal, fill=1.0,
                                    base=0, pattern=[[-1, P]], channel_multiplier=1).then_inc(s_const, 1)
            nc.gpsimd.affine_select(out=before[:, :], in_=before[:, :], compare_op=ALU.is_gt, fill=0.0,
                                    base=0, pattern=[[1, P]], channel_multiplier=-1).then_inc(s_const, 1)
            pool.wait_ge(s_slot, 1)


            def scatter(i, p):
                t = i * 2 + p
                if not isinstance(i, int):
                    pool.wait_ge(s_sc[p], i * (16 * R))
                nc.gpsimd.tensor_copy(idx_s[:, p, :], slot_i[:, ds(t * R, R)]).then_inc(s_stg, 1)
                nc.gpsimd.tensor_copy(rec_s[:, p, :, :], rec[:, ds(t * R, R), :]).then_inc(s_stg, 1)
                pool.wait_ge(s_stg, t * 2 + 2)
                pool.sem_inc(s_begun, 1)
                for u in range(R):
                    pool.indirect_dma_start(records, bass.IndirectOffsetOnAxis(ap=idx_s[:, p, u:u + 1], axis=0),
                                            rec_s[:, p, u, :], None).then_inc(s_sc[p], 16)

            scatter(0, 0)
            scatter(0, 1)
            with pool.Fori(1, TILES // R // 2, 1) as i:
                scatter(i, 0)
                scatter(i, 1)

            def gather(k, i, p):
                pool.wait_ge(s_idx[p], (i + (k * (TURNS // 2) + 1)) * 16)
                pool.sem_inc(s_begun, 1)
                for u in range(R):
                    pool.indirect_dma_start(got[:, p, u, :], None, table,
                                            bass.IndirectOffsetOnAxis(ap=idx_s[:, p, u:u + 1], axis=0)).then_inc(s_g[p], 16)

            for k in range(2):
                pool.wait_ge(s_tst, 16 * (k + 1))
                for p in range(2):
                    gather(k, 0, p)
                with pool.Fori(1, TURNS // 2, 1) as i:
                    for p in range(2):
                        gather(k, i, p)

        @block.scalar
        def _(act):
            def std(n):
                act.wait_ge(s_var, n)
                nc.scalar.activation(rstd[:, :], rstd[:, :], ACT.Sqrt).then_inc(s_std, 1)

            std(1)
            act.wait_ge(s_w, 16 * N_WEIGHTS)

            def silu1(s, u):
                act.wait_ge(s_mm1, s + 1)
                wait(act, s_mm2, s - 1)
                nc.scalar.activation(h1[:, u, :].rearrange("p (a b) -> p a b", a=2), ps[:, 2 * u:2 * u + 2, 0:CH // 2],
                                     ACT.Silu, bias=b1s[:, 0:1]).then_inc(s_h1, 1)

            def gate(s, u):
                act.wait_ge(s_mm2, s + 1)
                wait(act, s_msg, s - 1)
                v = ps[:, 4 + u, :].rearrange("p (q d) -> p q d", q=QT)
                nc.scalar.activation(sl[:, u, :, :], v[:, :, 0:D], ACT.Silu)
                nc.scalar.activation(th[:, u, :, :], v[:, :, D:2 * D], ACT.Tanh, scale=0.5).then_inc(s_sl, 1)

            silu1(0, 0)
            for s in range(1, R0):
                silu1(s, s % 2)
                gate(s - 1, (s - 1) % 2)
            with act.Fori(1, CSTEPS // R0, 1) as i:
                for u in range(R0):
                    silu1(i * R0 + u, u % 2)
                    gate(i * R0 + u - 1, (u - 1) % 2)
            gate(CSTEPS - 1, (CSTEPS - 1) % 2)

            at_n = [0]

            def linear(k):
                for g, pairs in enumerate(GROUPS):
                    for o in range(LINEARS[k]):
                        at_n[0] += 1
                        act.wait_ge(s_tp, at_n[0])
                        n = len(pairs) * P
                        nc.scalar.activation(at[:, g % 2, o, 0:n], ps[:, 2 * (g % 2) + o, 0:n], ACT.Copy).then_inc(s_at, 1)

            def weigh(i, p):
                act.wait_ge(s_wt, i * 2 + (p + 1))
                for u in range(R):
                    ins = nc.scalar.activation(oh[:, p, u, :], oh[:, p, u, :], ACT.Copy, scale=swgt[:, ds((i * 2 + p) * R + u, 1)])
                ins.then_inc(s_oh, 1)

            for k in range(PASSES):
                if k < 3:
                    std(2 + 2 * k if k < 2 else 6)
                    if k < 2:
                        act.wait_ge(s_var, 3 + 2 * k)
                        sc = scale1 if k == 0 else scale2
                        nc.scalar.activation(sc[:, :], sc[:, :], ACT.Sqrt).then_inc(s_std, 1)
                if k == 0:
                    linear(0)
                    for g in range(0, BSTEPS, SPAN):
                        act.wait_ge(s_pl, g // SPAN + 1)
                        m = min(SPAN, BSTEPS - g)
                        act.dma_start(places[0:1, g:g + m], tmp[4 + g // SPAN % 2][0:1, 0:m].bitcast(i32)).then_inc(s_pld[g // SPAN % 2], 16)
                    for p in range(2):
                        act.wait_ge(s_pld[p], 16 * ((-(-BSTEPS // SPAN) + 1 - p) // 2))
                    last = DEGREE_TURNS // 2
                    with act.Fori(1, last, 1) as i:
                        fetch(act, place_s, s_pls, i * 4 - 4, 4)
                        fetched(act, s_pls, i - 1)
                        for v in range(4):
                            write(act, place_s, i * 4 - 4 + v, v, 0, 0)
                    fetch(act, place_s, s_pls, UNITS0 - 4, 2)
                    act.wait_ge(s_pls, 16 * last)
                    for v in range(2):
                        write(act, place_s, UNITS0 - 4 + v, v, 0, 0)
                elif k == 1:
                    for p in range(2):
                        weigh(0, p)
                    with act.Fori(1, TURNS // 2, 1) as i:
                        n = i * 6 + (UNITS0 - 8)
                        fetch(act, place_s, s_pls, n, 6)
                        weigh(i, 0)
                        fetched(act, s_pls, i + (last - 1))
                        for v in range(3):
                            write(act, place_s, n + v, v, 0, 0)
                        weigh(i, 1)
                        for v in range(3, 6):
                            write(act, place_s, n + v, v, 0, 0)
                    fetch(act, place_s, s_pls, UNITS - 2, 2)
                    act.wait_ge(s_pls, 16 * FETCHES)
                    for v in range(2):
                        write(act, place_s, UNITS - 2 + v, v, 0, 0)
                    linear(k)
                else:
                    linear(k)

        @block.tensor
        def _(pe):
            pe.wait_ge(s_const, 6)
            pe.wait_ge(s_cnt, 1)
            nc.tensor.matmul(ps[:, 0, 0:NW], before[:, :], cnt[:, 0, :], start=True, stop=False)
            nc.tensor.matmul(ps[:, 0, 0:NW], ones[:, :], cex[:, 0, :], start=False, stop=True).then_inc(s_tot, 1)
            def blocks(i, p, first, last):
                pe.wait_ge(s_hp, i * 2 + (p + 1))
                for u in range(R):
                    ins = nc.tensor.matmul(ps[0:NW, 3, 0:NW], hone[:, p, 0, u, :], hone[:, p, 1, u, :], start=first and u == 0,
                                           stop=last and u == R - 1, skip_group_check=True)
                ins.then_inc(s_hm, 1)

            pe.wait_ge(s_cnt, 2)
            nc.tensor.matmul(ps[0:NW, 1, 0:1], cex[:, 0, :], ones[:, 0:1], start=True, stop=True)
            nc.tensor.matmul(ps[0:NW, 2, 0:1], cex[:, 1, :], ones[:, 0:1], start=True, stop=True).then_inc(s_tot, 1)
            blocks(0, 0, True, False)
            blocks(0, 1, False, False)
            with pe.Fori(1, TILES // R // 2, 1) as i:
                blocks(i, 0, False, False)
                blocks(i, 1, False, True)
            pe.wait_ge(s_bh, 1)
            for w in range(NW):
                ins = nc.tensor.matmul(ps[0:32, 0, 0:P], bhi[:, w, :], blo[:, w, :], start=w == 0, stop=w == NW - 1)
            ins.then_inc(s_bhm, 1)
            pe.wait_ge(s_pre, 1)
            nc.tensor.matmul(ps[0:32, 0, P:P + 1], before[0:32, 0:32], part[0:32, 0:1], start=True, stop=True).then_inc(s_prem, 1)
            for n, steps in enumerate((CSTEPS, TSTEPS, TSTEPS)):
                pe.wait_ge(s_wind, n + 1)
                nc.tensor.matmul(ps[0:1, 3, 0:NW], wst[:, 1:2], ident[0:NW, 0:NW], start=True, stop=True)
                for j in range(0, steps, 512):
                    m = min(512, steps - j)
                    last = nc.tensor.matmul(ps[0:1, 4 + j // 512, 0:m], ones[0:NW, 0:1], s2v[0:NW, TILES + j:TILES + j + m],
                                            start=True, stop=True)
                last.then_inc(s_wsum, 1)
            pe.wait_ge(s_w, 16 * N_WEIGHTS)
            pe.wait_ge(s_win, 3)
            pe.wait_ge(s_key, 1)

            def up(s, u):
                wait(pe, s_h1, s - 1)
                pe.wait_ge(s_xc[u], 16 * (s // R0 + 1) if isinstance(s, int) else (s - u) * (16 // R0) + 16)
                for h in range(2):
                    last = nc.tensor.matmul(ps[:, 2 * (u % 2) + h, 0:CH // 2], w1s[:, h, :],
                                            xs[:, u, :], start=True, stop=True)
                last.then_inc(s_mm1, 1)

            def mid(s, u):
                wait(pe, s_sl, s - 1)
                pe.wait_ge(s_h1, s + 1)
                nc.tensor.matmul(ps[:, 4 + u, :], onesb[:, :], b2b[:, :], start=True, stop=False)
                for q in range(QT):
                    last = nc.tensor.matmul(ps[:, 4 + u, q * P:(q + 1) * P], h1[:, u, q * P:(q + 1) * P], w2s[:, :],
                                            start=False, stop=q == QT - 1)
                last.then_inc(s_mm2, 1)

            def scat(s, u):
                pe.wait_ge(s_oh0, s + 1)
                pe.wait_ge(s_msg, s + 1)
                wait(pe, s_acc, s - 1)
                for q in range(QT):
                    last = nc.tensor.matmul(ps[:, 6 + u, 0:MW], oh0[:, u, q, :], msg[:, u, q, :],
                                            start=q == 0, stop=q == QT - 1)
                last.then_inc(s_scat, 1)

            up(0, 0)
            up(1, 1)
            mid(0, 0)
            for s in (2, 3):
                up(s, s)
                mid(s - 1, (s - 1) % 2)
                scat(s - 2, s % 2)
            with pe.Fori(1, CSTEPS // R0, 1) as i:
                for u in range(R0):
                    up(i * R0 + u, u)
                    mid(i * R0 + u - 1, (u - 1) % 2)
                    scat(i * R0 + u - 2, u % 2)
            mid(CSTEPS - 1, 1)
            scat(CSTEPS - 2, 0)
            scat(CSTEPS - 1, 1)

            def degree(i, p, first, last):
                pe.wait_ge(s_do, i * 2 + (p + 1))
                for u in range(R):
                    ins = nc.tensor.matmul(ps[:, 7, 0:NW], ohd[:, u, :], ohw[:, u, :], start=first and u == 0,
                                           stop=last and u == R - 1, skip_group_check=True)
                ins.then_inc(s_dm, 1)

            at_n, ev_n = [0], [0]

            def linear(k):
                ws = {0: [0], 1: [1], 2: [2, 3], 3: [4, 5]}[k]
                n_op = LINEARS[k]
                pe.wait_ge(s_op, k + 1)
                srcs = {0: [H], 1: [S1], 2: [S1, H], 3: [S1, H]}[k]

                def turn(g):
                    for o in range(n_op):
                        for j, pair in enumerate(GROUPS[g]):
                            last = nc.tensor.transpose(ps[:, 2 * (g % 2) + o, j * P:(j + 1) * P],
                                                       srcs[o][:, 2 * pair:2 * pair + 2, :].rearrange("p a b -> p (a b)"),
                                                       ident[:, :])
                        last.then_inc(s_tp, 1)

                turn(0)
                for g in range(len(GROUPS)):
                    if g + 1 < len(GROUPS):
                        turn(g + 1)
                    at_n[0] += n_op
                    pe.wait_ge(s_at, at_n[0])
                    if g >= 2:
                        pe.wait_ge(s_ev, ev_n[0] + g - 1)
                    for j in range(len(GROUPS[g])):
                        for o in range(n_op):
                            last = nc.tensor.matmul(ps[:, 4 + g % 2, j * P:(j + 1) * P], at[:, g % 2, o, j * P:(j + 1) * P],
                                                    wns[ws[o]][:, :], start=o == 0, stop=o == n_op - 1)
                    last.then_inc(s_y, 1)
                ev_n[0] += len(GROUPS)

            def add_up(k, i, p):
                pe.wait_ge(s_oh, i * 2 + (k * TURNS + p + 1))
                pe.wait_ge(s_g[p], i * (16 * R) + 16 * R * (k * (TURNS // 2) + 1))
                for u in range(R):
                    ins = nc.tensor.matmul(ps[:, 2 * p + u // 4, D * (u % 4):D * (u % 4 + 1)], oh[:, p, u, :], got[:, p, u, :],
                                           start=True, stop=True)
                ins.then_inc(s_mm, 1)

            def layout():
                pe.wait_ge(s_cast, 1)
                for k in range(3):
                    if k == 2:
                        pe.wait_ge(s_te, 1)
                    for c in range(TCH):
                        m = min(P, TILES - c * P)
                        last = nc.tensor.transpose(ps[0:m, 4 * (k % 2) + c // 4, c % 4 * P:c % 4 * P + P],
                                                   recf[:, c * P:c * P + m, k], ident[:, :])
                    last.then_inc(s_tr, 1)
                pe.wait_ge(s_te, 3)
                pe.wait_ge(s_ex, 1)
                for j in range(0, BSTEPS, 512):
                    m = min(512, BSTEPS - j)
                    last = nc.tensor.matmul(ps[:, j // 512, 0:m], ones[0:32, :], same[0:32, j:j + m], start=True, stop=True)
                last.then_inc(s_exm, 1)
                n_ex, n_sel = 1, 0
                for steps, keys in ((BSTEPS, 2), (TSTEPS, 3)):
                    for g in range(0, steps, SPAN):
                        m = min(SPAN, steps - g)
                        n_ex += 1
                        pe.wait_ge(s_ex, n_ex)
                        rows = 32 if keys == 2 else NW
                        nc.tensor.matmul(ps[:, 6, 0:m], ones[0:rows, :], tmp[3][0:rows, 0:m], start=True, stop=True).then_inc(s_exm, 1)
                        for c in range(TCH):
                            slot = n_sel % 3
                            n_sel += 1
                            pe.wait_ge(s_sel, n_sel)
                            for k in range(keys):
                                for j, of in enumerate(tile_parts[k]):
                                    last = nc.tensor.matmul(ps[:, k, 0:m], of[:, c * P:(c + 1) * P], sel[:, slot, 0:m],
                                                            start=c + j == 0, stop=c == TCH - 1 and j == len(tile_parts[k]) - 1,
                                                            skip_group_check=True)
                            last.then_inc(s_selm, 1)

            def unit(n, v):
                pe.wait_ge(s_bo, n + 1)
                wait(pe, s_bs, n * G - G)
                for j in range(G):
                    ins = nc.tensor.matmul(ps[:, 4 + v % 2, j * P:(j + 1) * P], bone[:, v % 2, :, j], bone[:, v % 2, :, G + j],
                                           start=True, stop=True)
                ins.then_inc(s_bm, 1)

            linear(0)
            layout()
            last = DEGREE_TURNS // 2
            add_up(0, 0, 0)
            add_up(0, 0, 1)
            unit(0, 0)
            unit(1, 1)
            degree(0, 0, True, False)
            with pe.Fori(1, last, 1) as i:
                for p in range(2):
                    add_up(0, i, p)
                    unit(i * 4 + (2 * p - 2), 0)
                    unit(i * 4 + (2 * p - 1), 1)
                    degree(i + (p - 1), 1 - p, False, False)
            add_up(0, last, 0)
            unit(UNITS0 - 2, 0)
            unit(UNITS0 - 1, 1)
            degree(last - 1, 1, False, True)
            add_up(0, last, 1)
            with pe.Fori(last + 1, TURNS // 2, 1) as i:
                for p in range(2):
                    add_up(0, i, p)
            for p in range(2):
                add_up(1, 0, p)
            with pe.Fori(1, TURNS // 2, 1) as i:
                for p in range(2):
                    n = i * 6 + (UNITS0 - 6 + 3 * p)
                    unit(n, p)
                    add_up(1, i, p)
                    unit(n + 1, p + 1)
                    unit(n + 2, p)
            linear(1)

            def group(kk, g, n):
                cols = SPAN if not isinstance(g, int) or g < DG else P
                for q, size in enumerate(PIECES):
                    pe.wait_ge(s_piece[q % 4], n * 32 + (16 * (q // 4) + 16))
                    if q == 0:
                        wait(pe, s_gs, n)
                    for v in range(size):
                        ins = nc.tensor.matmul(ps[0:D, 6, 0:cols], H[:, 6 * q + v, :], pieces[q % 4][:, v * cols:(v + 1) * cols],
                                               start=q + v == 0, stop=6 * q + v == NW - 1, skip_group_check=True)
                    ins.then_inc(s_pd, 1)
                pe.wait_ge(s_gs, n + 1)
                wait(pe, s_gb, n)
                pe.sem_inc(s_turned, 1)
                for j in range(cols // P):
                    ins = nc.tensor.transpose(ps[:, 7, j * D:(j + 1) * D], agg_t[:, j * P:(j + 1) * P], ident[0:D, 0:D])
                ins.then_inc(s_gt, 1)

            for kk in range(2):
                pe.wait_ge(s_tab, 3 + kk)
                first = kk * (DG + 1)
                group(kk, 0, first)
                with pe.Fori(1, DG, 1) as g:
                    group(kk, g, g + first)
                group(kk, DG, DG + first)
                linear(2 + kk)

        @block.vector
        def _(dve):
            chain = [0]

            def link(ins):
                chain[0] += 1
                ins.then_inc(s_v, 1)
                dve.wait_ge(s_v, chain[0])

            V = nc.vector
            dve.wait_ge(s_const, 6)
            dve.wait_ge(s_rows, 48)
            link(V.tensor_single_scalar(tmp_i, srow_i, 7, op=ALU.logical_shift_right))
            link(V.tensor_copy(hi_f[:, :], tmp_i))
            link(V.tensor_single_scalar(tmp_i, srow_i, P - 1, op=ALU.bitwise_and))
            link(V.tensor_copy(lo_f[:, :], tmp_i))
            link(V.memset(recf[:, :, 3:4], 0.0))
            V.tensor_copy(rec[:, :, 0:1].rearrange("p t a -> p (t a)"), srow_i)
            V.tensor_copy(rec[:, :, 1:2].rearrange("p t a -> p (t a)"), drow_i)
            link(V.tensor_copy(recf[:, :, 2:3].rearrange("p t a -> p (t a)"), wrow))
            count_n = [0]

            def tally(key):
                n = count_n[0]
                with dve.Fori(0, NW, 1) as w:
                    V.tensor_scalar(mask, key, wcol[:, ds(w, 1)], None, ALU.is_equal, ALU.add,
                                    accum_out=cnt[:, n, ds(w, 1)]).then_inc(s_v, 1)
                    dve.wait_ge(s_v, w + (chain[0] + 1))
                chain[0] += NW
                link(V.memset(cex[:, n, 0:1], 0.0))
                V.tensor_tensor_scan(cex[:, n, 1:NW], ones[:, 0:NW - 1], cnt[:, n, 0:NW - 1], 0.0,
                                     ALU.mult, ALU.add).then_inc(s_cnt, 1)
                count_n[0] += 1
                dve.wait_ge(s_cnt, n + 1)

            tally(hi_f[:, :])
            dve.wait_ge(s_tot, 1)
            link(V.tensor_copy(base[:, :], ps[:, 0, 0:NW]))
            with dve.Fori(0, NW, 1) as w:
                n0 = chain[0]
                V.tensor_scalar(mask, hi_f[:, :], wcol[:, ds(w, 1)], None, ALU.is_equal).then_inc(s_v, 1)
                dve.wait_ge(s_v, w * 3 + (n0 + 1))
                V.tensor_tensor_scan(run, ones[:, 0:1].broadcast_to([P, TILES]), mask, base[:, ds(w, 1)],
                                     ALU.mult, ALU.add).then_inc(s_v, 1)
                dve.wait_ge(s_v, w * 3 + (n0 + 2))
                dve.sem_inc(s_placed, 1)
                V.copy_predicated(pos, mask.bitcast(i32), run).then_inc(s_v, 1)
                dve.wait_ge(s_v, w * 3 + (n0 + 3))
            chain[0] += 3 * NW
            link(V.tensor_scalar(tmp_i, pos, -1.0, None, ALU.add))
            link(V.tensor_single_scalar(slot_i[:, :], tmp_i, P - 1, op=ALU.bitwise_and))
            link(V.tensor_single_scalar(srow_i, tmp_i, 7, op=ALU.logical_shift_right))
            V.scalar_tensor_tensor(out=slot_i[:, :], in0=slot_i[:, :], scalar=float(TILES), in1=srow_i,
                                   op0=ALU.mult, op1=ALU.add).then_inc(s_slot, 1)
            dve.wait_ge(s_slot, 1)
            link(V.tensor_single_scalar(tmp_i, drow_i, 7, op=ALU.logical_shift_right))
            link(V.tensor_copy(pos, tmp_i))
            tally(pos)
            dve.wait_ge(s_tot, 2)
            wide3 = lambda v: v.rearrange("p (r a) -> p r a", a=1).broadcast_to([P, R, NW])
            wcol_r = wcol[:, :].rearrange("p (a n) -> p a n", a=1).broadcast_to([P, R, NW])

            def blocks(i, p):
                t = i * 2 + p
                wait(dve, s_hm, t - 1)
                V.tensor_tensor(hone[:, p, 0, :, :], wcol_r, wide3(hi_f[:, ds(t * R, R)]), ALU.is_equal)
                V.tensor_tensor(hone[:, p, 1, :, :], wcol_r, wide3(pos[:, ds(t * R, R)]), ALU.is_equal).then_inc(s_hp, 1)

            blocks(0, 0)
            blocks(0, 1)
            with dve.Fori(1, TILES // R // 2, 1) as i:
                blocks(i, 0)
                blocks(i, 1)
            dve.wait_ge(s_hm, TILES // R)
            link(V.tensor_copy(cex[0:NW, 0, :], ps[0:NW, 3, 0:NW]))
            link(V.memset(cex[0:NW, 1, 0:1], 0.0))
            link(V.tensor_tensor_scan(cex[0:NW, 1, 1:NW], ones[0:NW, 0:NW - 1], cex[0:NW, 0, 0:NW - 1], 0.0, ALU.mult, ALU.add))
            link(V.tensor_copy(wst[:, 0:1], ps[0:NW, 1, 0:1]))
            bt_i = base[0:NW, :].bitcast(i32)
            link(V.tensor_scalar(bt_i, cex[0:NW, 1, :], wst[:, 0:1], None, ALU.add))
            link(V.tensor_single_scalar(bt_i, bt_i, 7, op=ALU.logical_shift_right))
            link(V.tensor_copy(cex[0:NW, 0, :], bt_i))
            link(V.tensor_scalar(cex[0:NW, 0, :], cex[0:NW, 0, :], float(TILES - 1), None, ALU.min))
            link(V.tensor_scalar(cex[0:NW, 1, :], wcol[0:NW, :], 1.0, None, ALU.mult))
            link(V.tensor_scalar(part[0:NW, 0:1], pidx[0:NW, :], float(NW), None, ALU.mult))
            link(V.tensor_scalar(cex[0:NW, 1, :], cex[0:NW, 1, :], part[0:NW, 0:1], None, ALU.add))
            link(V.tensor_tensor(bt_i, cex[0:NW, 0, :], cex[0:NW, 1, :], ALU.add))
            step_i = wfirst[0:NW, :].bitcast(i32)
            link(V.tensor_single_scalar(step_i, bt_i, P - 1, op=ALU.bitwise_and))
            link(V.tensor_copy(cex[0:NW, 0, :], step_i))
            link(V.tensor_single_scalar(step_i, bt_i, 7, op=ALU.logical_shift_right))
            link(V.tensor_copy(cex[0:NW, 1, :], step_i))
            V.tensor_tensor(blo, iota[0:NW, 0:P].rearrange("p (a n) -> p a n", a=1).broadcast_to([NW, NW, P]),
                            cex[0:NW, 0, :].rearrange("p (r a) -> p r a", a=1).broadcast_to([NW, NW, P]), ALU.is_equal)
            V.tensor_tensor(bhi, iota[0:NW, 0:32].rearrange("p (a n) -> p a n", a=1).broadcast_to([NW, NW, 32]),
                            cex[0:NW, 1, :].rearrange("p (r a) -> p r a", a=1).broadcast_to([NW, NW, 32]),
                            ALU.is_equal).then_inc(s_bh, 1)
            dve.wait_ge(s_bhm, 1)
            link(V.tensor_copy(mark[:, :], ps[0:32, 0, 0:P]))
            link(V.tensor_tensor_scan(block_at[:, :], ones[0:32, :], mark[:, :], 0.0, ALU.mult, ALU.add))
            V.tensor_copy(part[0:32, 0:1], block_at[:, P - 1:P]).then_inc(s_pre, 1)
            dve.wait_ge(s_prem, 1)
            link(V.tensor_copy(part[0:32, 1:2], ps[0:32, 0, P:P + 1]))
            link(V.tensor_scalar(block_at[:, :], block_at[:, :], part[0:32, 1:2], -1.0, ALU.add, ALU.add))
            for j in range(ROWS // 4 * 4 + TCH):
                V.tensor_scalar(parts[:, j:j + 1], pidx[:, :], float(P * (j - ROWS // 4 * 4)), None, ALU.add)
            for n, (bank, shift, last) in enumerate(((2, 9, CHUNKS - 1), (2, 7, TILES - 1), (1, 7, TILES - 1))):
                link(V.tensor_copy(wst_i[:, 0:1], ps[0:NW, bank, 0:1]))
                link(V.tensor_single_scalar(wst_i[:, 1:2], wst_i[:, 0:1], shift, op=ALU.logical_shift_right))
                link(V.tensor_copy(wst[:, 0:1], wst_i[:, 1:2]))
                link(V.tensor_scalar(wst[:, 1:2], wst[:, 0:1], float(last), pidx[0:NW, :], ALU.min, ALU.add))
                steps = CSTEPS if n == 0 else TSTEPS
                V.tensor_scalar(s2v[0:NW, TILES:TILES + steps], iota[0:NW, 0:steps], wst[:, 1:2], None,
                                ALU.is_ge).then_inc(s_wind, 1)
                dve.wait_ge(s_wsum, n + 1)
                if n < 2:
                    V.tensor_copy(wbeg[n][:, :], ps[0:1, 3, 0:NW])
                tab = (dwin_c, dwin_t, swin_t)[n]
                for j in range(0, steps, 512):
                    m = min(512, steps - j)
                    ins = V.tensor_single_scalar(tab[:, j:j + m], ps[0:1, 4 + j // 512, 0:m], -1.0, op=ALU.add)
                ins.then_inc(s_win, 1)
                dve.wait_ge(s_win, n + 1)

            def relay(w, n, q, steps, key):
                s = load(dve, wbeg[n][0:1, ds(w, 1)], steps // q - 1)[0]
                t = less(s, w, TILES // q - 1)
                to, of = s1v[:, ds(s * q, TILES)], s2v[:, ds(t * q, TILES)]
                if key:
                    ins = V.tensor_scalar(to, of, wfirst[:, ds(w, 1)], None, ALU.add)
                else:
                    ins = V.tensor_copy(to, of)
                ins.then_inc(s_lay, 1)

            link(V.tensor_single_scalar(wfirst[:, :], wcol[:, :], -float(P), op=ALU.mult))
            V.memset(s1v[:, 2 * TILES:WIDE], 0.0)
            link(V.memset(s2v[:, TILES:WIDE], 0.0))
            dve.wait_ge(s_dt, 16)
            link(V.tensor_copy(s2v[:, 0:TILES], dtile_i))
            with dve.Fori(0, NW, 1) as w:
                relay(w, 0, QT, CSTEPS * QT, True)
                dve.wait_ge(s_lay, w + 1)
            link(V.tensor_copy(dkey_c[:, :], s1v[:, 0:CSTEPS * QT]))
            dve.wait_ge(s_w, 16 * N_WEIGHTS)
            for j in range(3):
                link(V.tensor_scalar(part[:, j:j + 1], pidx[:, :], float(j), None, ALU.is_equal))
            link(V.memset(b2u, 0.0))
            for j in range(3):
                link(V.tensor_copy(b2b[:, :], b2s))
                link(V.tensor_copy(b2t, b2b[:, :]))
                link(V.scalar_tensor_tensor(out=b2u, in0=b2t, scalar=part[:, j:j + 1], in1=b2u, op0=ALU.mult, op1=ALU.add))
                link(V.tensor_tensor(b2s, b2s, b2t, ALU.subtract))
            link(V.tensor_copy(b2b[:, :], b2u))
            V.memset(onesb[:, :], 1.0)
            V.memset(msg[:, :, :, D:MW], 1.0).then_inc(s_key, 1)

            var_n = [0]
            bc = lambda t: t[:, :].rearrange("p (w a) -> p w a", a=1).broadcast_to([P, NWP, D])

            def layernorm():
                link(V.tensor_reduce(mean[:, :], X[:, :, :], axis=AX.X, op=ALU.add))
                link(V.tensor_single_scalar(mean[:, :], mean[:, :], 1.0 / D, op=ALU.mult))
                link(V.tensor_tensor(H[:, :, :], X[:, :, :], bc(mean), ALU.subtract))
                link(V.tensor_tensor(S2[:, :, :], H[:, :, :], H[:, :, :], ALU.mult))
                link(V.tensor_reduce(rstd[:, :], S2[:, :, :], axis=AX.X, op=ALU.add))
                V.tensor_scalar(rstd[:, :], rstd[:, :], 1.0 / D, EPS, ALU.mult, ALU.add).then_inc(s_var, 1)
                var_n[0] += 1
                dve.wait_ge(s_std, var_n[0])
                link(V.reciprocal(rstd[:, :], rstd[:, :]))
                link(V.scalar_tensor_tensor(out=H[:, :, :], in0=H[:, :, :], scalar=0.0, in1=bc(rstd),
                                            op0=ALU.max, op1=ALU.mult))

            dve.wait_ge(s_x, 16)
            layernorm()
            link(V.memset(ACC[:, :, :], 0.0))

            iota_q = iota[:, 0:P].rearrange("p (a n) -> p a n", a=1)

            def onehots(s, u):
                wait(dve, s_scat, s - 1)
                V.tensor_tensor(oh0[:, u, :, :], iota_q.broadcast_to([P, QT, P]),
                                dkey_c[:, ds(s * QT, QT)].rearrange("p (q a) -> p q a", a=1).broadcast_to([P, QT, P]),
                                ALU.is_equal).then_inc(s_oh0, 1)

            def message(s, u):
                dve.wait_ge(s_sl, s + 1)
                wait(dve, s_scat, s - 1)
                V.scalar_tensor_tensor(out=msg[:, u, :, 0:D], in0=th[:, u, :, :], scalar=1.0, in1=sl[:, u, :, :],
                                       op0=ALU.add, op1=ALU.mult).then_inc(s_msg, 1)

            def add_chunk(s, u, w):
                dve.wait_ge(s_scat, s + 1)
                wait(dve, s_acc, s)
                to = accv[:, ds(w * MW, MW)]
                V.tensor_tensor(to, to, ps[:, 6 + u, 0:MW], ALU.add).then_inc(s_acc, 1)

            onehots(0, 0)
            onehots(1, 1)
            message(0, 0)
            w = windows(dve, dwin_c, 0, R0)
            for s in (2, 3):
                add_chunk(s - 2, s % 2, w[s - 2])
                onehots(s, s % 2)
                message(s - 1, (s - 1) % 2)

            def four(i):
                w = windows(dve, dwin_c, i * R0 - 2, R0)
                for u in range(R0):
                    add_chunk(i * R0 + u - 2, u % 2, w[u])
                    onehots(i * R0 + u, u % 2)
                    message(i * R0 + u - 1, (u - 1) % 2)

            link(V.tensor_copy(s2v[:, 0:TILES], dtile_i))
            with dve.Fori(1, NW + 1, 1) as i:
                four(i)
                dve.wait_ge(s_lay, i + (NW - 1))
                relay(i - 1, 1, 1, TSTEPS, True)
            dve.wait_ge(s_lay, 2 * NW)
            link(V.tensor_copy(dkey[:, :], s1v[:, 0:TSTEPS]))
            dve.wait_ge(s_st, 16)
            link(V.tensor_copy(s2v[:, 0:TILES], stile_i))
            with dve.Fori(NW + 1, 2 * NW + 1, 1) as i:
                four(i)
                dve.wait_ge(s_lay, i + (NW - 1))
                relay(i - (NW + 1), 1, 1, TSTEPS, False)
            dve.wait_ge(s_lay, 3 * NW)
            link(V.tensor_copy(dget[:, :], s1v[:, 0:TSTEPS]))
            with dve.Fori(2 * NW + 1, CSTEPS // R0, 1) as i:
                four(i)
            w = windows(dve, dwin_c, CSTEPS - 2, 2)
            add_chunk(CSTEPS - 2, 0, w[0])
            message(CSTEPS - 1, 1)
            add_chunk(CSTEPS - 1, 1, w[1])

            def degree(i, p):
                t = i * 2 + p
                wait(dve, s_dm, t)
                wide = lambda v, n: v.rearrange("p (r a) -> p r a", a=1).broadcast_to([P, R, n])
                V.tensor_tensor(ohd, iota_q.broadcast_to([P, R, P]), wide(lo_f[:, ds(t * R, R)], P), ALU.is_equal)
                V.tensor_tensor(ohw[:, :, :], wcol[:, :].rearrange("p (a n) -> p a n", a=1).broadcast_to([P, R, NW]),
                                wide(hi_f[:, ds(t * R, R)], NW), ALU.is_equal).then_inc(s_dp, 1)
                dve.wait_ge(s_dp, t + 1)
                V.tensor_tensor(ohw[:, :, :], ohw[:, :, :], wide(wgt[:, ds(t * R, R)], NW), ALU.mult).then_inc(s_do, 1)

            dve.wait_ge(s_acc, CSTEPS)
            dve.wait_ge(s_scat, CSTEPS)
            V.tensor_copy(wgt, recf[:, :, 2:3].rearrange("p t a -> p (t a)")).then_inc(s_kept, 1)
            dve.wait_ge(s_kept, 1)
            link(V.tensor_copy(count[:, :], ACC[:, :, D]))
            link(V.tensor_tensor(X[:, :, :], X[:, :, :], H[:, :, :], ALU.add))
            link(V.scalar_tensor_tensor(out=X[:, :, :], in0=ACC[:, :, 0:D], scalar=0.5, in1=X[:, :, :],
                                        op0=ALU.mult, op1=ALU.add))
            layernorm()

            y_n = [0]

            def products(evac):
                for g, pairs in enumerate(GROUPS):
                    y_n[0] += 1
                    dve.wait_ge(s_y, y_n[0])
                    w0, nw = 2 * pairs[0], 2 * len(pairs)
                    yv = ps[:, 4 + g % 2, 0:nw * D].rearrange("p (w d) -> p w d", d=D)
                    evac(slice(w0, w0 + nw), nw, yv).then_inc(s_ev, 1)
                dve.wait_ge(s_ev, y_n[0])

            def degrees(sc, deg):
                link(V.tensor_scalar(mean[:, :], deg, 0.0, None, ALU.is_gt))
                link(V.tensor_tensor(sc[:, :], deg, mean[:, :], ALU.mult))
                link(V.scalar_tensor_tensor(out=sc[:, :], in0=mean[:, :], scalar=-1.0, in1=sc[:, :],
                                            op0=ALU.mult, op1=ALU.add))
                V.tensor_scalar(sc[:, :], sc[:, :], 1.0, None, ALU.add).then_inc(s_var, 1)
                var_n[0] += 1
                dve.wait_ge(s_std, var_n[0])
                link(V.reciprocal(sc[:, :], sc[:, :]))
                link(V.tensor_tensor(sc[:, :], sc[:, :], mean[:, :], ALU.mult))

            bias = lambda b, nw: b[:, :].rearrange("p (a d) -> p a d", a=1).broadcast_to([P, nw, D])

            def layout():
                dve.wait_ge(s_rec, 16)
                for k in range(2):
                    ins = V.tensor_copy(recf[:, :, k:k + 1], rec[:, :, k:k + 1])
                ins.then_inc(s_cast, 1)
                dve.wait_ge(s_tst, 16)
                link(V.memset(tt[:, :, TCH - 1:TCH, :], 0.0))
                for k in range(3):
                    dve.wait_ge(s_tr, k + 1)
                    b, full = 4 * (k % 2), TCH // 4 * 4
                    V.tensor_copy(tt[:, k, 0:full, :].rearrange("p c e -> p (c e)"),
                                  ps[:, b:b + TCH // 4, :].rearrange("p a b -> p (a b)"))
                    m = TILES - full * P
                    V.tensor_copy(tt[0:m, k, full, :], ps[0:m, b + TCH // 4, 0:P]).then_inc(s_te, 1)
                dve.wait_ge(s_te, 3)
                a1, a2 = ring[:, 0:TCH * P], H[:, 0:TCH * P // D, :].rearrange("p a b -> p (a b)")
                for k in range(2):
                    v = tt[:, k, :, :].rearrange("p c e -> p (c e)")
                    link(V.tensor_copy(a1.bitcast(i32), v))
                    link(V.tensor_single_scalar(a1.bitcast(i32), a1.bitcast(i32), P - 1, op=ALU.bitwise_and))
                    link(V.tensor_copy(a2, a1.bitcast(i32)))
                    link(V.tensor_tensor(a1, v, a2, ALU.subtract))
                    V.tensor_copy(tile_parts[k][0], a2)
                    link(V.tensor_copy(tile_parts[k][1], a1))
                v = tt[:, 2, :, :].rearrange("p c e -> p (c e)")
                link(V.tensor_copy(third, v))
                link(V.tensor_copy(a1, third))
                link(V.tensor_tensor(a2, v, a1, ALU.subtract))
                link(V.tensor_copy(tile_parts[2][0], a1))
                link(V.tensor_copy(third, a2))
                link(V.tensor_copy(a1, third))
                link(V.tensor_tensor(a2, a2, a1, ALU.subtract))
                link(V.tensor_copy(tile_parts[2][1], a1))
                link(V.tensor_copy(third, a2))

                def spanned(rows, table, h, n):
                    return (rows.rearrange("p (h n) -> p h n", n=P), table[:, :].rearrange("p (a n) -> p a n", a=1).broadcast_to([32, n, P]),
                            ident[0:32, h:h + n].rearrange("p (h a) -> p h a", a=1).broadcast_to([32, n, P]), ALU.mult)

                V.tensor_tensor(*spanned(same[0:32, 0:BSTEPS], mark, 0, ROWS)).then_inc(s_ex, 1)
                dve.wait_ge(s_exm, 1)
                link(V.memset(same[:, BSTEPS:BSTEPS + 1], 0.0))
                for j in range(0, BSTEPS, 512):
                    m = min(512, BSTEPS - j)
                    ins = V.tensor_scalar(same[:, j:j + m], ps[:, j // 512, 0:m], -1.0, 1.0, ALU.mult, ALU.add)
                link(ins)
                n_ex, n_sel = 1, 0
                t_tile, t_a, t_b, t_rows = tmp[0:4]
                a_i, b_i = t_a.bitcast(i32), t_b.bitcast(i32)
                for steps, keys in ((BSTEPS, 2), (TSTEPS, 3)):
                    for g in range(0, steps, SPAN):
                        m = min(SPAN, steps - g)
                        n_ex += 1
                        e = ps[:, 6, 0:m]
                        if keys == 2:
                            V.tensor_tensor(*spanned(t_rows[0:32, 0:m], block_at, g // P, m // P)).then_inc(s_ex, 1)
                            dve.wait_ge(s_exm, n_ex)
                            link(V.scalar_tensor_tensor(out=t_tile[:, 0:m], in0=e, scalar=-1.0, in1=iota[:, 0:m],
                                                        op0=ALU.mult, op1=ALU.add))
                            col = ROWS // 4 * 4 - g // P
                        else:
                            V.tensor_scalar(t_rows[0:NW, 0:m], iota[0:NW, g:g + m], wst[:, 1:2], None, ALU.is_ge).then_inc(s_ex, 1)
                            dve.wait_ge(s_exm, n_ex)
                            link(V.tensor_scalar(t_a[:, 0:m], e, -1.0, None, ALU.add))
                            link(V.scalar_tensor_tensor(out=t_tile[:, 0:m], in0=t_a[:, 0:m], scalar=-1.0, in1=iota[:, g:g + m],
                                                        op0=ALU.mult, op1=ALU.add))
                            col = ROWS // 4 * 4
                        for c in range(TCH):
                            wait(dve, s_selm, n_sel - 2)
                            n_sel += 1
                            V.tensor_scalar(sel[:, (n_sel - 1) % 3, 0:m], t_tile[:, 0:m], parts[:, col + c:col + c + 1], None,
                                            ALU.is_equal).then_inc(s_sel, 1)
                        if keys == 2:
                            link(V.tensor_copy(a_i[:, 0:m], e))
                            link(V.tensor_single_scalar(a_i[:, 0:m], a_i[:, 0:m], OVER, op=ALU.mult))
                            link(V.tensor_single_scalar(a_i[:, 0:m], a_i[:, 0:m], 16, op=ALU.logical_shift_right))
                            link(V.tensor_copy(t_b[:, 0:m], a_i[:, 0:m]))
                            link(V.scalar_tensor_tensor(out=t_a[:, 0:m], in0=t_b[:, 0:m], scalar=-float(NW), in1=e,
                                                        op0=ALU.mult, op1=ALU.add))
                            dve.wait_ge(s_selm, n_sel)
                            for k, window in ((0, t_b), (1, t_a)):
                                u = 0
                                while u < m // G:
                                    u0 = g // G + u
                                    tab = int(u0 >= UNITS0)
                                    n = min(m // G - u, (UNITS if tab else UNITS0) - u0)
                                    to = bkey[tab][:, u0 - tab * UNITS0:u0 - tab * UNITS0 + n, G * k:G * k + G]
                                    by = lambda v: v[:, u * G:(u + n) * G].rearrange("p (u j) -> p u j", j=G)
                                    ins = V.scalar_tensor_tensor(out=to, in0=by(window), scalar=-float(P), in1=by(ps[:, k, :]),
                                                                 op0=ALU.mult, op1=ALU.add)
                                    u += n
                            link(ins)
                            spare = s12[:, sel_at:sel_at + m]
                            spare_i = spare.bitcast(i32)
                            link(V.tensor_copy(spare_i, iota[:, 0:m]))
                            link(V.tensor_single_scalar(spare_i, spare_i, 2 * G - 1, op=ALU.bitwise_and))
                            link(V.tensor_single_scalar(spare, spare_i, 4.0 * P, op=ALU.mult))
                            place = tmp[4 + g // SPAN % 2]
                            four_i, four = t_rows[:, 0:m].bitcast(i32), t_tile[:, 0:m]
                            link(V.tensor_copy(four_i, t_a[:, 0:m]))
                            link(V.tensor_single_scalar(four_i, four_i, 2, op=ALU.logical_shift_right))
                            link(V.tensor_copy(four, four_i))
                            link(V.scalar_tensor_tensor(out=t_a[:, 0:m], in0=four, scalar=float(4 * P * NW - 4), in1=t_a[:, 0:m],
                                                        op0=ALU.mult, op1=ALU.add))
                            link(V.scalar_tensor_tensor(out=t_a[:, 0:m], in0=t_b[:, 0:m], scalar=float(4 * P), in1=t_a[:, 0:m],
                                                        op0=ALU.mult, op1=ALU.add))
                            link(V.scalar_tensor_tensor(out=t_a[:, 0:m], in0=t_a[:, 0:m], scalar=-float(SPARE), in1=spare,
                                                        op0=ALU.add, op1=ALU.subtract))
                            link(V.tensor_tensor(t_rows[:, 0:m], same[:, g + 1:g + 1 + m], t_a[:, 0:m], ALU.mult))
                            link(V.tensor_tensor(t_a[:, 0:m], t_a[:, 0:m], t_rows[:, 0:m], ALU.subtract))
                            wait(dve, s_pld[g // SPAN % 2], g // SPAN // 2 * 16)
                            V.scalar_tensor_tensor(out=place[:, 0:m].bitcast(i32), in0=t_a[:, 0:m], scalar=float(SPARE),
                                                   in1=spare, op0=ALU.add, op1=ALU.add).then_inc(s_pl, 1)
                            dve.wait_ge(s_pl, g // SPAN + 1)
                        else:
                            link(V.tensor_scalar(t_a[:, 0:m], t_a[:, 0:m], -float(P), None, ALU.mult))
                            dve.wait_ge(s_selm, n_sel)
                            V.tensor_tensor(skey[:, g:g + m], ps[:, 0, 0:m], t_a[:, 0:m], ALU.add)
                            V.tensor_copy(sget[:, g:g + m], ps[:, 1, 0:m])
                            link(V.tensor_copy(swgt[:, g:g + m], ps[:, 2, 0:m]))
                V.tensor_copy(bone_iota, iota[:, 0:P].rearrange("p (n a) -> p n a", a=1).broadcast_to([P, P, 2 * G]))
                link(V.memset(sums[:, 1, G - 1:G, :], 0.0))


            def unit_ones(n, v, tab):
                wait(dve, s_bm, n - 1)
                V.tensor_tensor(bone[:, v % 2, :, :], bone_iota,
                                bkey[tab][:, ds(n - tab * UNITS0, 1), :].broadcast_to([P, P, 2 * G]),
                                ALU.is_equal).then_inc(s_bo, 1)

            def unit_wait(n, v):
                dve.wait_ge(s_bm, n + 1)
                if isinstance(n, int):
                    wait(dve, s_bw[v % 2], n // 2 * (16 * G))
                else:
                    dve.wait_ge(s_bw[v % 2], (n - (v % 2)) * (8 * G))

            def unit_step(n, v, j):
                wait(dve, s_bs, n * G + j)
                prev = sums[:, v % 2, j - 1, :] if j else sums[:, (v + 1) % 2, G - 1, :]
                V.scalar_tensor_tensor(out=sums[:, v % 2, j, :], in0=prev, scalar=same[:, ds(n * G + j, 1)],
                                       in1=ps[:, 4 + v % 2, j * P:(j + 1) * P], op0=ALU.mult, op1=ALU.add).then_inc(s_bs, 1)

            def spread(k):
                tab_of = swin_t if k == 1 else dwin_t
                key = skey if k == 1 else dkey

                def onehot(i, p):
                    t = i * 2 + p
                    wait(dve, s_mm, k * TURNS + i * 2 + p - 1)
                    wide = lambda v: v.rearrange("p (r a) -> p r a", a=1).broadcast_to([P, R, P])
                    ins = V.tensor_tensor(oh[:, p, :, :], iota_q.broadcast_to([P, R, P]), wide(key[:, ds(t * R, R)]),
                                          ALU.is_equal)
                    ins.then_inc(s_oh if k == 0 else s_wt, 1)

                def add(i, p, n=None, units=(), tab=0):
                    t = i * 2 + p
                    turn = i * 2 + (k * TURNS + p + 1)
                    if not isinstance(i, int):
                        turn = dve.snap(turn)
                    w = windows(dve, tab_of, t * R, R)
                    dve.wait_ge(s_mm, turn)
                    share = -(-R // len(units)) if units else R
                    for u in range(R):
                        v = u // share
                        if units and u % share == 0:
                            unit_ones(n + v, units[v], tab)
                            if not isinstance(n, int) or n + v > 1:
                                unit_wait(n + v - 2, units[v])
                        wait(dve, s_add[u - 1], turn if u else turn - 1)
                        to = ACC[:, ds(w[u], 1), 0:D].rearrange("p a b -> p (a b)")
                        V.tensor_tensor(to, to, ps[:, 2 * p + u // 4, D * (u % 4):D * (u % 4 + 1)], ALU.add).then_inc(s_add[u], 1)
                        if units and (not isinstance(n, int) or n + v > 1):
                            unit_step(n + v - 2, units[v], u % share)
                            last = u == R - 1 or u % share == share - 1
                            for j in range(u % share + 1, G if last else 0):
                                unit_step(n + v - 2, units[v], j)

                onehot(0, 0)
                onehot(0, 1)
                if k == 0:
                    add(0, 0, 0, (0, 1))
                    degree(0, 0)
                    with dve.Fori(1, DEGREE_TURNS // 2, 1) as i:
                        onehot(i, 0)
                        add(i - 1, 1, i * 4 - 2, (0, 1))
                        degree(i - 1, 1)
                        onehot(i, 1)
                        add(i, 0, i * 4, (0, 1))
                        degree(i, 0)
                    last = DEGREE_TURNS // 2
                    onehot(last, 0)
                    add(last - 1, 1, last * 4 - 2, (0, 1))
                    degree(last - 1, 1)
                    onehot(last, 1)
                    add(last, 0)
                    with dve.Fori(last + 1, TURNS // 2, 1) as i:
                        onehot(i, 0)
                        add(i - 1, 1)
                        onehot(i, 1)
                        add(i, 0)
                    add(TURNS // 2 - 1, 1)
                else:
                    add(0, 0)
                    with dve.Fori(1, TURNS // 2, 1) as i:
                        n = i * 6 + (UNITS0 - 6)
                        onehot(i, 0)
                        add(i - 1, 1, n, (0, 1, 2), 1)
                        onehot(i, 1)
                        add(i, 0, n + 3, (3, 4, 5), 1)
                    add(TURNS // 2 - 1, 1)
                    for v in range(2):
                        unit_wait(UNITS - 2 + v, v)
                        for j in range(G):
                            unit_step(UNITS - 2 + v, v, j)
                dve.wait_ge(s_add[R - 1], (k + 1) * TURNS)

            link(V.tensor_scalar(scale3[:, :], count[:, :], 1.0, None, ALU.add))
            degrees(scale1, scale3[:, :])
            V.memset(scale3[:, 0:1], 0.0).then_inc(s_op, 1)
            sc1 = lambda ww, nw: scale1[:, ww].rearrange("p (w a) -> p w a", a=1).broadcast_to([P, nw, D])
            products(lambda ww, nw, y: V.tensor_tensor(S1[:, ww, :], y, sc1(ww, nw), ALU.mult))
            V.tensor_copy(ACC[:, :, 0:D], S1[:, :, :]).then_inc(s_tab, 1)
            layout()
            spread(0)
            link(V.tensor_tensor(S1[:, :, :], ACC[:, :, 0:D], bc(scale1), ALU.mult))
            link(V.tensor_tensor(S1[:, :, :], S1[:, :, :], bias(bns[0], NWP), ALU.add))
            link(V.scalar_tensor_tensor(out=X[:, :, :], in0=S1[:, :, :], scalar=0.0, in1=X[:, :, :],
                                        op0=ALU.max, op1=ALU.add))
            layernorm()
            dve.wait_ge(s_dm, DEGREE_TURNS)
            link(V.memset(scale3[:, :], 1.0))
            link(V.tensor_scalar(scale3[:, 0:NW], ps[:, 7, 0:NW], 1.0, None, ALU.add))
            degrees(scale2, scale3[:, :])
            link(V.tensor_tensor(S1[:, :, :], H[:, :, :], bc(scale2), ALU.mult))
            V.tensor_copy(ACC[:, :, 0:D], S1[:, :, :]).then_inc(s_tab, 1)
            spread(1)
            V.tensor_tensor(S1[:, :, :], ACC[:, :, 0:D], bc(scale2), ALU.mult).then_inc(s_op, 1)
            dve.wait_ge(s_op, 2)
            link(V.tensor_tensor(X[:, :, :], X[:, :, :], bias(bns[1], NWP), ALU.add))
            products(lambda ww, nw, y: V.tensor_tensor(X[:, ww, :], X[:, ww, :], y, ALU.add))
            layernorm()
            link(V.tensor_scalar(scale3[:, :], count[:, :], 1.0, None, ALU.max))
            link(V.reciprocal(scale3[:, :], scale3[:, :]))
            V.memset(S1[:, NW:NWP, :], 0.0).then_inc(s_tab, 1)
            dve.wait_ge(s_tab, 3)

            def means(kk):
                def group(g, n):
                    ws = 4 if not isinstance(g, int) or g < DG else 1
                    dve.wait_ge(s_pd, n * 8 + 8)
                    wait(dve, s_gt, n)
                    V.tensor_copy(agg_t[:, 0:ws * P], ps[0:D, 6, 0:ws * P]).then_inc(s_gs, 1)
                    dve.wait_ge(s_gt, n + 1)
                    V.tensor_tensor(S1[:, ds(g * 4, ws), :], ps[:, 7, 0:ws * D].rearrange("p (w d) -> p w d", d=D),
                                    scale3[:, ds(g * 4, ws)].rearrange("p (w a) -> p w a", a=1).broadcast_to([P, ws, D]),
                                    ALU.mult).then_inc(s_gb, 1)

                first = kk * (DG + 1)
                group(0, first)
                with dve.Fori(1, DG, 1) as g:
                    group(g, g + first)
                group(DG, DG + first)
                dve.wait_ge(s_gb, first + DG + 1)
                V.memset(mean[:, 0:1], 0.0).then_inc(s_op, 1)

            means(0)
            products(lambda ww, nw, y: V.tensor_tensor(S2[:, ww, :], y, bias(bns[2], nw), ALU.add))
            link(V.tensor_scalar(H[:, :, :], S2[:, :, :], 0.0, None, ALU.max))
            V.memset(mean[:, 0:1], 0.0).then_inc(s_tab, 1)
            means(1)
            link(V.tensor_tensor(X[:, :, :], X[:, :, :], bias(bns[3], NWP), ALU.add))
            products(lambda ww, nw, y: V.tensor_tensor(X[:, ww, :], X[:, ww, :], y, ALU.add))
            V.memset(mean[:, 0:1], 0.0).then_inc(s_fin, 1)


def kernel(**inputs):
    import numpy as np
    import concourse.bacc as bacc
    from concourse.bass_utils import run_bass_kernel_spmd as run

    def a(name):
        return np.ascontiguousarray(inputs[name])

    def padded(v, fill):
        return np.concatenate([v, np.full((EDGES - N_EDGES,), fill, v.dtype)])

    def twice(w):
        both = np.zeros((P, P), w.dtype)
        both[0:D, 0:D] = w
        both[D:P, D:P] = w
        return both

    def rows(b):
        return np.ascontiguousarray(np.broadcast_to(b, (P, D)))

    x = np.zeros((NWP * P, D), np.float32)
    x[0:N_NODES] = a("x")
    e = np.zeros((EDGES, D), np.float32)
    e[0:N_EDGES] = a("edge_attr_64")
    src, dst = padded(a("src"), DUMMY), padded(a("dst"), DUMMY)
    w = padded(a("edge_weight"), 0)
    w2g2 = np.zeros((P, P), np.float32)
    w2g2[0:D, 0:D] = a("L0_gnn_W2")
    w2g2[D:P, D:P] = a("L0_gnn_G2")
    zero = np.zeros((D, P), np.float32)
    w1g1 = np.concatenate([a("L0_gnn_W1"), a("L0_gnn_G1")], axis=1)
    arrays = {
        "x": x.reshape(NWP, P, D).transpose(1, 0, 2),
        "edge_t": e.reshape(CHUNKS, 2, CH // 2, D).transpose(0, 1, 3, 2).reshape(CHUNKS, P, CH // 2),
        "dst_tiles": dst.reshape(TILES, P).T, "src_tiles": src.reshape(TILES, P).T,
        "src_rows": src.reshape(P, TILES), "dst_rows": dst.reshape(P, TILES), "w_rows": w.reshape(P, TILES),
        "w1g1": np.stack([np.concatenate([w1g1, zero]), np.concatenate([zero, w1g1])], axis=1).reshape(P, 2 * P),
        "w2g2": w2g2,
        "b1g1": np.concatenate([a("L0_gnn_b1"), a("L0_gnn_g1")]).reshape(P, 1),
        "b2g2": np.tile(np.concatenate([a("L0_gnn_b2"), a("L0_gnn_g2")]), (P, QT)),
        "w_gcn": twice(a("L1_gnn_W")), "w_l2": twice(a("L2_gnn_W").T),
        "w_l0": twice(a("L3_gnn_Wl0")), "w_r0": twice(a("L3_gnn_Wr0")),
        "w_l1": twice(a("L3_gnn_Wl1")), "w_r1": twice(a("L3_gnn_Wr1")),
        "b_gcn": rows(a("L1_gnn_b")), "b_l2": rows(a("L2_gnn_b")),
        "b_l0": rows(a("L3_gnn_bl0")), "b_l1": rows(a("L3_gnn_bl1")),
    }
    nc = bacc.Bacc("TRN2", target_bir_lowering=False, num_devices=1)
    sent, args = {}, []
    for name, v in arrays.items():
        sent[f"in_{name}"] = np.ascontiguousarray(v)
        args.append(nc.dram_tensor(f"in_{name}", v.shape, mybir.dt.from_np(v.dtype), kind="ExternalInput").ap())
    args.append(nc.dram_tensor("out_0", (N_NODES, D), mybir.dt.float32, kind="ExternalOutput").ap())
    gnn_kernel(nc, *args)
    return run(nc, [sent], core_ids=[0]).results[0]["out_0"]
```
